# Optimizing a Trainium2 kernel written in Bass

```python
import numpy as np
import jax
import jax.numpy as jnp

def _softmax(x, axis=-1):
    return jax.nn.softmax(x, axis=axis)

def _gelu(x):
    return jax.nn.gelu(x, approximate=True)

def _silu(x):
    return jax.nn.silu(x)

def _sigmoid(x):
    return jax.nn.sigmoid(x)

def _layernorm(x, axis=-1, eps=1e-05):
    m = jnp.mean(x, axis=axis, keepdims=True)
    v = jnp.var(x, axis=axis, keepdims=True)
    return (x - m) / jnp.sqrt(v + eps)

def _scatter_add(tgt, idx, src, axis=0):
    return tgt.at[idx].add(src)

def _segment_sum(src, seg, n):
    return jax.ops.segment_sum(src, seg, n)
kernel_name = 'mk_macaron_d1_jaxref_r8_e65a92'

def setup_inputs(seed: int=0):
    np.random.seed(seed)
    _w = jnp.asarray

    def _L0_attn_setup():
        import jax, jax.numpy as jnp
        import numpy as np
        HEADS = 16

        def _split_heads(t, h):
            b, y, hd = t.shape
            d = hd // h
            return t.reshape(b, y, h, d).transpose(0, 2, 1, 3).reshape(b * h, y, d)

        def _merge_heads(t, b, h):
            bh, y, d = t.shape
            return t.reshape(b, h, y, d).transpose(0, 2, 1, 3).reshape(b, y, h * d)
        key = jax.random.key(seed)
        ks = jax.random.split(key, 5)
        B, S, D = (8, 512, 128)
        scale = 1.0 / np.sqrt(D)
        x = jax.random.normal(ks[0], (B, S, D), dtype=jnp.float32)
        Wq = jax.random.normal(ks[1], (D, D), dtype=jnp.float32) * scale
        Wk = jax.random.normal(ks[2], (D, D), dtype=jnp.float32) * scale
        Wv = jax.random.normal(ks[3], (D, D), dtype=jnp.float32) * scale
        Wo = jax.random.normal(ks[4], (D, D), dtype=jnp.float32) * scale
        return {'x': x, 'Wq': Wq, 'Wk': Wk, 'Wv': Wv, 'Wo': Wo}
    _L0_attn_in = _L0_attn_setup()

    def _L0_ffn_setup():
        import jax, jax.numpy as jnp
        import numpy as np
        B, S, H = (4, 256, 128)
        E, K = (8, 2)
        I_R, I_S = (4 * H, 8 * H)
        CAP_FACTOR = 1.25
        SCALE = 1.0
        key = jax.random.key(seed)
        ks = jax.random.split(key, 9)
        std = 0.02
        return {'x': jax.random.normal(ks[0], (B, S, H), jnp.float32), 'router_w': std * jax.random.normal(ks[1], (E, H), jnp.float32), 'rg': std * jax.random.normal(ks[2], (E, H, I_R), jnp.float32), 'ru': std * jax.random.normal(ks[3], (E, H, I_R), jnp.float32), 'rd': std * jax.random.normal(ks[4], (E, I_R, H), jnp.float32), 'sg': std * jax.random.normal(ks[5], (H, I_S), jnp.float32), 'su': std * jax.random.normal(ks[6], (H, I_S), jnp.float32), 'sd': std * jax.random.normal(ks[7], (I_S, H), jnp.float32)}
    _L0_ffn_in = _L0_ffn_setup()
    _d = {'L0_attn_x': _L0_attn_in['x'], 'L0_attn_Wq': _L0_attn_in['Wq'], 'L0_attn_Wk': _L0_attn_in['Wk'], 'L0_attn_Wv': _L0_attn_in['Wv'], 'L0_attn_Wo': _L0_attn_in['Wo'], 'L0_ffn_router_w': _L0_ffn_in['router_w'], 'L0_ffn_rg': _L0_ffn_in['rg'], 'L0_ffn_ru': _L0_ffn_in['ru'], 'L0_ffn_rd': _L0_ffn_in['rd'], 'L0_ffn_sg': _L0_ffn_in['sg'], 'L0_ffn_su': _L0_ffn_in['su'], 'L0_ffn_sd': _L0_ffn_in['sd']}
    _x0 = _d['L0_attn_x']
    _d['L0_attn_x'] = jax.random.normal(jax.random.fold_in(jax.random.key(seed), 1), (8, 256, 128), dtype=_x0.dtype)
    del _x0
    return _d

def reference(L0_attn_x, L0_attn_Wq, L0_attn_Wk, L0_attn_Wv, L0_attn_Wo, L0_ffn_router_w, L0_ffn_rg, L0_ffn_ru, L0_ffn_rd, L0_ffn_sg, L0_ffn_su, L0_ffn_sd):

    def _L0_attn_ref(x, Wq, Wk, Wv, Wo):
        import jax, jax.numpy as jnp
        import numpy as np
        HEADS = 16

        def _split_heads(t, h):
            b, y, hd = t.shape
            d = hd // h
            return t.reshape(b, y, h, d).transpose(0, 2, 1, 3).reshape(b * h, y, d)

        def _merge_heads(t, b, h):
            bh, y, d = t.shape
            return t.reshape(b, h, y, d).transpose(0, 2, 1, 3).reshape(b, y, h * d)
        b = x.shape[0]
        h = HEADS
        q = _split_heads(x @ Wq.T, h)
        k = _split_heads(x @ Wk.T, h)
        v = _split_heads(x @ Wv.T, h)
        d = q.shape[-1]
        z = jnp.einsum('byq,byk->bkq', q, k) / jnp.sqrt(jnp.asarray(d, x.dtype))
        z = jax.nn.softmax(z, axis=-1)
        z = jnp.einsum('byz,bvy->bvz', z, v)
        z = _merge_heads(z, b, h)
        return z @ Wo.T

    def _L0_ffn_ref(x, router_w, rg, ru, rd, sg, su, sd):
        import jax, jax.numpy as jnp
        import numpy as np
        B, S, H = (4, 256, 128)
        E, K = (8, 2)
        I_R, I_S = (4 * H, 8 * H)
        CAP_FACTOR = 1.25
        SCALE = 1.0
        b, s, h = x.shape
        T = b * s
        capacity = max(int(CAP_FACTOR * T / E), 1)
        xf = x.reshape(T, h)
        eps = jnp.finfo(x.dtype).eps
        xn = xf * jax.lax.rsqrt(jnp.mean(xf * xf, axis=-1, keepdims=True) + eps)
        logits = xn @ router_w.T
        probs = jax.nn.softmax(logits, axis=-1)
        topk_p, topk_i = jax.lax.top_k(probs, K)
        rw = topk_p / jnp.sum(topk_p, axis=-1, keepdims=True)
        one_hot = jax.nn.one_hot(topk_i, E, dtype=x.dtype)
        mask = one_hot.sum(1)
        wdense = (one_hot * rw[..., None]).sum(1)
        sel = mask.T.astype(bool)
        order = jnp.argsort(~sel, axis=1, stable=True)
        dispatch = order[:, :capacity]
        count = sel.sum(axis=1)
        valid = (jnp.arange(capacity)[None, :] < count[:, None]).astype(x.dtype)
        xg = xf[dispatch]
        gate = jax.nn.silu(jnp.einsum('ech,ehi->eci', xg, rg))
        up = jnp.einsum('ech,ehi->eci', xg, ru)
        eout = jnp.einsum('eci,eih->ech', gate * up, rd)
        w = jnp.take_along_axis(wdense.T, dispatch, axis=1)
        contrib = eout * (w * valid)[..., None]
        routed = jnp.zeros_like(xf).at[dispatch.reshape(-1)].add(contrib.reshape(-1, h))
        shared = jax.nn.silu(x @ sg) * (x @ su) @ sd
        return shared + SCALE * routed.reshape(b, s, h)
    x = L0_attn_x
    x = x + 0.5 * _L0_ffn_ref(_layernorm(x, axis=-1), L0_ffn_router_w, L0_ffn_rg, L0_ffn_ru, L0_ffn_rd, L0_ffn_sg, L0_ffn_su, L0_ffn_sd)
    x = x + _L0_attn_ref(_layernorm(x, axis=-1), L0_attn_Wq, L0_attn_Wk, L0_attn_Wv, L0_attn_Wo)
    x = x + 0.5 * _L0_ffn_ref(_layernorm(x, axis=-1), L0_ffn_router_w, L0_ffn_rg, L0_ffn_ru, L0_ffn_rd, L0_ffn_sg, L0_ffn_su, L0_ffn_sd)
    return x

_drawn_inputs = setup_inputs


def setup_inputs(seed=0):
    import zlib

    import numpy as np

    out = dict(_drawn_inputs(seed))
    spreads = {}
    factors = {'L0_ffn_router_w': 8.0,
     'L0_ffn_rg': 8.0,
     'L0_ffn_ru': 8.0,
     'L0_ffn_rd': 8.0,
     'L0_ffn_sg': 3.635,
     'L0_ffn_su': 3.592,
     'L0_ffn_sd': 3.624}
    for name, (base, spread) in spreads.items():
        noise = np.random.default_rng([zlib.crc32(name.encode()), seed]).standard_normal(out[name].shape)
        drawn = base * np.exp(spread * noise) if base else spread * noise
        out[name] = jnp.asarray(drawn.astype(out[name].dtype))
    for name, factor in factors.items():
        out[name] = (out[name] * factor).astype(out[name].dtype)
    return out
```

```python
from contextlib import ExitStack

import concourse.bass as bass
from concourse import mybir

ALU = mybir.AluOpType
ACT = mybir.ActivationFunctionType
AX = mybir.AxisListType
F32 = mybir.dt.float32
F32R = mybir.dt.float32r
BF16 = mybir.dt.bfloat16
U32 = mybir.dt.uint32

P = 128


def macaron_block_kernel(nc, x, w_gate_up, w_down, w_attn, w_router, consts, out):
    T, H = x.shape
    LAYERS = 2
    E = w_router.shape[1]
    HT = w_down.shape[1] // P
    HT_EXPERT = 4 * H // P
    HT_SHARED = HT - E * HT_EXPERT
    CAP = max(int(1.25 * T / E), 1)
    TILES = T // P
    TPC = 4
    CHUNKS = TILES // TPC
    C = TPC * P
    SEQ = 2 * P
    BPC = C // SEQ
    HEAD = 8
    TOP = 2
    BLOCKS = [(j * P, min(P, CAP - j * P)) for j in range((CAP + P - 1) // P)]
    NB = len(BLOCKS)
    ROW = H + 4
    COL_ID, COL_E0, COL_W1, COL_DW = H, H + 1, H + 2, H + 3
    FAR = 4096
    LN_EPS = 1e-5
    RMS_EPS = 1.1920928955078125e-07
    SCALE = float(HEAD) ** -0.5
    HPP = 2
    PIECES = HT // HPP
    PIECE = HPP * 2 * P
    RAW_RING, XG_RING, H_RING, XA_RING = 4, 3, 3, 3

    SHARED, EXPERT = "shared", "expert"
    order = [[(SHARED, 0), (SHARED, 1)] + [(EXPERT, e) for e in range(E)] + [(SHARED, 2), (SHARED, 3)],
             [(SHARED, 0), (SHARED, 1), (SHARED, 2)] + [(EXPERT, e) for e in range(E)] + [(SHARED, 3)]]
    units, slots, first_slot, last_slot = [], [], {}, {}
    for l in range(LAYERS):
        for kind, i in order[l]:
            u = len(units)
            units.append((kind, l, i))
            tiles = HT_SHARED if kind == SHARED else HT_EXPERT
            base = 0 if kind == SHARED else HT_SHARED + i * HT_EXPERT
            first_slot[u] = len(slots)
            for k in range(tiles):
                slots.append((u, k, tiles, base + k, C if kind == SHARED else CAP))
            last_slot[u] = len(slots) - 1
    unit_of = {v: u for u, v in enumerate(units)}
    NSLOT = len(slots)

    stages = {}

    def at(slot, name, arg):
        stages.setdefault(slot, []).append((name, arg))

    for name in ("ln", "apply", "transpose"):
        at(-1, name, 0)
    for p in (0, 1):
        at(-1, "split", p)
    at(1, "split", 2)
    at(3, "split", 3)
    for slot, name, q in ((0, "route", 0), (0, "ln", 1), (0, "ln", 2), (1, "ln", 3), (1, "rank", 0),
                          (1, "apply", 1), (1, "transpose", 1), (2, "route", 1), (2, "apply", 2),
                          (3, "transpose", 2), (3, "rank", 1), (4, "route", 2), (4, "apply", 3),
                          (5, "transpose", 3), (5, "rank", 2), (6, "route", 3), (7, "rank", 3)):
        at(slot, name, q)
    for p in range(4, PIECES):
        at(p, "split", p)
    for u, (kind, l, i) in enumerate(units):
        at(last_slot[u] + 2, "out_copy", u)
        at(last_slot[u] + 3, "out_turn", u)
        if kind == EXPERT:
            at(first_slot[u] - (1 if i == 0 else 2), "gathered", (l, i))
    for c, s in enumerate((53, 54, 59, 67)):
        for d, name in ((0, "combine"), (1, "a_apply"), (1, "a_turn"), (2, "a_gram"), (3, "a_gq"), (4, "a_kq"),
                        (5, "a_soft"), (6, "a_pv"), (7, "a_mix"), (8, "a_out")):
            at(s + d, name, c)
        for d, name in ((8, "ln"), (9, "apply"), (9, "transpose"), (11, "route"), (12, "rank")):
            at(s + d, name, CHUNKS + c)
    for c, s in enumerate((125, 126, 127, 130)):
        at(s, "finish", c)
    LAST = max(stages)

    with ExitStack() as ctx:
        def sb(name, shape, dt=F32):
            return ctx.enter_context(nc.sbuf_tensor(name, shape, dt))

        def pb(name, shape):
            return ctx.enter_context(nc.psum_tensor(name, shape, F32))

        def sem(name):
            return ctx.enter_context(nc.semaphore(name))

        rows_dram = [nc.dram_tensor(f"rows_{l}", [E * CAP, ROW], F32, kind="Internal").ap() for l in range(LAYERS)]
        sums_dram = [nc.dram_tensor(f"sums_{l}", [T + P, H], F32, kind="Internal").ap() for l in range(LAYERS)]

        cst = sb("cst", [P, 3 * P])
        ident, block_mask = cst[:, 0:P], cst[:, P:2 * P]
        wa = sb("wa", [P, 4 * P])
        wqT, wkT, wv, woT = (wa[:, i * P:(i + 1) * P] for i in range(4))
        wr = sb("wr", [P, E])
        tri = sb("tri", [P, P], BF16)
        ones = sb("ones", [P, P], BF16)
        iota_e = sb("iota_e", [P, E])
        slot_base = sb("slot_base", [P, E])
        mhalf = sb("mhalf", [P, 2, TPC])
        init_row = sb("init_row", [P, ROW])
        zeros = sb("zeros", [P, C])

        raw = sb("raw", [P, RAW_RING, PIECE])
        wgu_hi = sb("wgu_hi", [P, HT * 2 * P], F32R)
        wgu_lo = sb("wgu_lo", [P, HT * 2 * P], F32R)
        wd = sb("wd", [P, HT * P])

        X = sb("X", [P, TILES, H])
        XN = sb("XN", [P, TILES, ROW])
        xT_hi = sb("xT_hi", [P, CHUNKS, C], F32R)
        xT_lo = sb("xT_lo", [P, CHUNKS, C], F32R)
        S = sb("S", [P, 2, C])
        Hd = sb("Hd", [P, H_RING, C])
        oT = sb("oT", [P, C])
        xg = sb("xg", [P, XG_RING, NB, ROW])
        xgT_hi = sb("xgT_hi", [P, 2, CAP], F32R)
        xgT_lo = sb("xgT_lo", [P, 2, CAP], F32R)
        wsl = sb("wsl", [P, XG_RING, NB])
        yw = sb("yw", [P, 2, NB, H])
        sums = sb("sums", [P, 2, TPC, H])

        NLN = (LAYERS + 1) * CHUNKS
        stat = sb("stat", [P, NLN, TPC, 6])
        mv = sb("mv", [P, NLN, TPC, 2])
        var_eps = sb("var_eps", [P, NLN, TPC])
        pow_in = sb("pow_in", [P, NLN, 2, TPC])
        pow_out = sb("pow_out", [P, NLN, 2, TPC])
        logit = sb("logit", [P, TPC, E])
        top_v = sb("top_v", [P, 2, TPC, 8])
        top_i = sb("top_i", [P, 2, TPC, 8], U32)
        choice = sb("choice", [P, 2, TOP, TPC, E])
        mask = sb("mask", [P, 2, TPC, E], BF16)
        seen = sb("seen", [P, 2, E], BF16)
        seen_c = sb("seen_c", [P, E])
        gap = sb("gap", [P, 2, TPC])
        tanh_gap = sb("tanh_gap", [P, 2, TPC])
        late = sb("late", [P, TPC, E])
        place = sb("place", [P, TPC, E])
        picked = sb("picked", [P, TOP, TPC, E])
        place_f = sb("place_f", [P, TOP, TPC])
        place_u = sb("place_u", [P, LAYERS * CHUNKS, TOP, TPC], U32)

        xaT = sb("xaT", [P, XA_RING, C])
        gram = sb("gram", [P, 2, BPC, P])
        gq = sb("gq", [P, 2, BPC, P])
        kq = sb("kq", [P, BPC, P])
        zc = sb("zc", [P, BPC, HEAD])
        zmax = sb("zmax", [P, BPC])
        zs = sb("zs", [P, 2, BPC, HEAD])
        zt = sb("zt", [P, 2, BPC, HEAD])
        znum = sb("znum", [P, BPC, HEAD])
        zden = sb("zden", [P, BPC, HEAD])
        zsum = sb("zsum", [P, BPC])
        zb = sb("zb", [P, 2, BPC, P])
        pv = sb("pv", [P, 2, BPC, P])
        mix = sb("mix", [P, 2, BPC, P])

        psG = [pb(f"psG{i}", [P, C]) for i in range(2)]
        psU = [pb(f"psU{i}", [P, C]) for i in range(2)]
        psD = [pb(f"psD{i}", [P, C]) for i in range(2)]
        psM = [pb(f"psM{i}", [P, C]) for i in range(2)]

        const_in = sem("const_in")
        x_in = [sem(f"x_in{c}") for c in range(CHUNKS)]
        attn_in = sem("attn_in")
        down_in = [sem(f"down_in{i}") for i in range(2)]
        raw_in = [sem(f"raw_in{i}") for i in range(RAW_RING)]
        hi_split, lo_split = sem("hi_split"), sem("lo_split")
        bf_ready = sem("bf_ready")
        pool_const, dve_const = sem("pool_const"), sem("dve_const")
        init_done = sem("init_done")
        gu_done, silu_done, hidden_done, down_done = sem("gu_done"), sem("silu_done"), sem("hidden_done"), sem("down_done")
        out_copied, out_turned = sem("out_copied"), sem("out_turned")
        out_read, logits_read, ranks_read = sem("out_read"), sem("logits_read"), sem("ranks_read")
        kq_read, attn_added = sem("kq_read"), sem("attn_added")
        dve_step, pool_step = sem("dve_step"), sem("pool_step")
        ln_stats, ln_pow, xn_done = sem("ln_stats"), sem("ln_pow"), sem("xn_done")
        an_stats, an_pow, xa_done = sem("an_stats"), sem("an_pow"), sem("xa_done")
        xT_turned, xT_hi_done, xT_lo_done = sem("xT_turned"), sem("xT_hi_done"), sem("xT_lo_done")
        logits_done, masks_done, gap_done, tanh_done = sem("logits_done"), sem("masks_done"), sem("gap_done"), sem("tanh_done")
        ranks_done, places_done = sem("ranks_done"), sem("places_done")
        dispatched = [sem(f"dispatched{l}") for l in range(LAYERS)]
        rows_in = [sem(f"rows_in{i}") for i in range(XG_RING)]
        xg_turned, xg_hi_done, xg_lo_done = sem("xg_turned"), sem("xg_hi_done"), sem("xg_lo_done")
        added = sem("added")
        sums_in = [sem(f"sums_in{i}") for i in range(2)]
        combined = sem("combined")
        xa_turned, xaT_done = sem("xa_turned"), sem("xaT_done")
        gram_ps, gram_sb, gq_ps, gq_sb, kq_ps = sem("gram_ps"), sem("gram_sb"), sem("gq_ps"), sem("gq_sb"), sem("kq_ps")
        zs_done, zt_done, zb_done = sem("zs_done"), sem("zt_done"), sem("zb_done")
        pv_ps, pv_sb, mix_ps, mix_sb, attn_ps = sem("pv_ps"), sem("pv_sb"), sem("mix_ps"), sem("mix_sb"), sem("attn_ps")
        stored = sem("stored")

        x_t = x.rearrange("(t p) h -> p t h", p=P)
        out_t = out.rearrange("(t p) h -> p t h", p=P)

        def tiles_of(c):
            return slice(c * TPC, (c + 1) * TPC)

        def gidx(l, e):
            return l * E + e

        def raw_ready(eng, p):
            eng.wait_ge(raw_in[p % RAW_RING], 16 * (p // RAW_RING + 1))

        block = ctx.enter_context(nc.Block())

        @block.sync
        def _(sp):
            def piece(p):
                if p >= RAW_RING:
                    sp.wait_ge(lo_split, p - RAW_RING + 1)
                sp.dma_start(raw[:, p % RAW_RING, :], w_gate_up[:, p * PIECE:(p + 1) * PIECE])\
                    .then_inc(raw_in[p % RAW_RING], 16)

            sp.dma_start(X[:, tiles_of(0), :], x_t[:, tiles_of(0), :]).then_inc(x_in[0], 16)
            piece(0)
            sp.dma_start(X[:, tiles_of(1), :], x_t[:, tiles_of(1), :]).then_inc(x_in[1], 16)
            sp.dma_start(X[:, tiles_of(2), :], x_t[:, tiles_of(2), :]).then_inc(x_in[2], 16)
            piece(1)
            sp.dma_start(wd[:, 0:HT_SHARED * P], w_down[:, 0:HT_SHARED * P]).then_inc(down_in[0], 16)
            sp.dma_start(X[:, tiles_of(3), :], x_t[:, tiles_of(3), :]).then_inc(x_in[3], 16)
            piece(2)
            sp.wait_ge(pool_const, 2)
            sp.wait_ge(dve_const, 1)
            for l in range(LAYERS):
                sp.dma_start(rows_dram[l].rearrange("(i p) c -> p i c", p=P),
                             init_row[:].unsqueeze(1).to_broadcast([P, E * CAP // P, ROW])).then_inc(init_done, 16)
            piece(3)
            for l in range(LAYERS):
                for c in range(CHUNKS):
                    sp.dma_start(sums_dram[l][c * C:(c + 1) * C, :].rearrange("(p t) h -> p (t h)", p=P), zeros[:])\
                        .then_inc(init_done, 16)
                sp.dma_start(sums_dram[l][T:T + P, :], zeros[:, 0:H]).then_inc(init_done, 16)
            sp.dma_start(wa[:], w_attn).then_inc(attn_in, 16)
            piece(4)
            sp.dma_start(wd[:, HT_SHARED * P:], w_down[:, HT_SHARED * P:]).then_inc(down_in[1], 16)
            for p in range(5, PIECES):
                piece(p)
            for l in range(LAYERS):
                for e in range(E):
                    g = gidx(l, e)
                    if e == 0:
                        sp.wait_ge(dispatched[l], 16 * TOP * TILES)
                    if g >= XG_RING:
                        sp.wait_ge(added, 16 * NB * (g - XG_RING + 1))
                    full = CAP // P
                    sp.dma_start(xg[:, g % XG_RING, 0:full, :],
                                 rows_dram[l][e * CAP:e * CAP + full * P, :].rearrange("(j p) c -> p j c", p=P))\
                        .then_inc(rows_in[g % XG_RING], 16)
                    for r0, n in BLOCKS[full:]:
                        sp.dma_start(xg[0:n, g % XG_RING, full, :],
                                     rows_dram[l][e * CAP + r0:e * CAP + r0 + n, :]).then_inc(rows_in[g % XG_RING], 16)
                sp.wait_ge(added, 16 * NB * E * (l + 1))
                for c in range(CHUNKS):
                    k = l * CHUNKS + c
                    if k >= 2:
                        sp.wait_ge(combined, k - 1)
                    sp.dma_start(sums[:, k % 2, :, :],
                                 sums_dram[l][c * C:(c + 1) * C, :].rearrange("(t p) h -> p t h", p=P))\
                        .then_inc(sums_in[k % 2], 16)
            for c in range(CHUNKS):
                sp.wait_ge(combined, CHUNKS + c + 1)
                sp.dma_start(out_t[:, tiles_of(c), :], X[:, tiles_of(c), :]).then_inc(stored, 16)
            sp.wait_ge(stored, 16 * CHUNKS)

        @block.tensor
        def _(pe):
            reader = [None, None]

            def take(bank, *read):
                if reader[bank]:
                    pe.wait_ge(*reader[bank])
                reader[bank] = read
                return psM[bank]

            def gate_up(n):
                u, k, tiles, ht, N = slots[n]
                kind, l, i = units[u]
                if n >= 2:
                    pe.wait_ge(hidden_done, n - 1)
                if l == 0 and (kind == EXPERT or i == 0):
                    pe.wait_ge(lo_split, ht // HPP + 1)
                if k == 0:
                    if kind == SHARED:
                        pe.wait_ge(xT_lo_done, l * CHUNKS + i + 1)
                    else:
                        pe.wait_ge(xg_lo_done, gidx(l, i) + 1)
                if kind == SHARED:
                    hi, lo = xT_hi[:, i, :], xT_lo[:, i, :]
                else:
                    hi, lo = xgT_hi[:, gidx(l, i) % 2, :], xgT_lo[:, gidx(l, i) % 2, :]
                for half, ps in ((0, psG[n % 2]), (1, psU[n % 2])):
                    o = (2 * ht + half) * P
                    pe.matmul(ps[:, 0:N], wgu_hi[:, o:o + P], hi, start=True, stop=False)
                    pe.matmul(ps[:, 0:N], wgu_hi[:, o:o + P], lo, start=False, stop=False)
                    mm = pe.matmul(ps[:, 0:N], wgu_lo[:, o:o + P], hi, start=False, stop=True)
                mm.then_inc(gu_done, 1)

            def down(n):
                u, k, tiles, ht, N = slots[n]
                pe.wait_ge(hidden_done, n + 1)
                if k == 0 and u >= 2:
                    pe.wait_ge(out_copied, u - 1)
                if u == 0 and k == 0:
                    pe.wait_ge(down_in[0], 16)
                if units[u][0] == EXPERT and k == 0:
                    pe.wait_ge(down_in[1], 16)
                pe.matmul(psD[u % 2][:, 0:N], wd[:, ht * P:(ht + 1) * P], Hd[:, n % H_RING, 0:N],
                          start=(k == 0), stop=(k == tiles - 1)).then_inc(down_done, 1)

            def transpose(q):
                c = q % CHUNKS
                ps = take(0, xT_lo_done, q + 1)
                pe.wait_ge(xn_done, q + 1)
                for t in range(TPC):
                    mm = pe.transpose(ps[:, t * P:(t + 1) * P], XN[:, c * TPC + t, 0:H], ident)
                mm.then_inc(xT_turned, 1)

            def route(q):
                c = q % CHUNKS
                pe.wait_ge(xT_lo_done, q + 1)
                ps = take(1, logits_read, q + 1)
                for t in range(TPC):
                    for part, buf in enumerate((xT_hi, xT_lo)):
                        mm = pe.matmul(ps[:, t * E:(t + 1) * E], buf[:, c, t * P:(t + 1) * P].bitcast(F32), wr[:],
                                       start=(part == 0), stop=(part == 1))
                mm.then_inc(logits_done, 1)

            def rank(q):
                c = q % CHUNKS
                pe.wait_ge(masks_done, q + 1)
                ps = take(1, ranks_read, q + 1)
                m = mask[:, q % 2]
                mm = pe.matmul(ps[:, 0:TPC * E], tri[:], m.rearrange("p t e -> p (t e)"), start=True, stop=True)
                for d in range(1, TPC):
                    mm = pe.matmul(ps[:, d * E:TPC * E], ones[:], m[:, 0:TPC - d, :].rearrange("p t e -> p (t e)"),
                                   start=False, stop=True, skip_group_check=True)
                if c:
                    mm = pe.matmul(ps[:, 0:TPC * E], ones[:], seen[:, q % 2].unsqueeze(1).to_broadcast([P, TPC, E]),
                                   start=False, stop=True, skip_group_check=True)
                mm.then_inc(ranks_done, 1)

            def gathered(le):
                g = gidx(*le)
                ps = take(0, xg_lo_done, g + 1)
                pe.wait_ge(rows_in[g % XG_RING], 32 * (g // XG_RING + 1))
                for j, (r0, n) in enumerate(BLOCKS):
                    mm = pe.transpose(ps[:, r0:r0 + n], xg[0:n, g % XG_RING, j, 0:H], ident[0:n, 0:n])
                mm.then_inc(xg_turned, 1)

            def out_turn(u):
                kind, l, i = units[u]
                ps = take(1, out_read, u + 1)
                pe.wait_ge(out_copied, u + 1)
                if kind == SHARED:
                    for t in range(TPC):
                        mm = pe.transpose(ps[:, t * P:(t + 1) * P], oT[:, t * P:(t + 1) * P], ident)
                else:
                    for j, (r0, n) in enumerate(BLOCKS):
                        mm = pe.transpose(ps[0:n, j * P:(j + 1) * P], oT[:, r0:r0 + n], ident)
                mm.then_inc(out_turned, 1)

            def a_turn(c):
                ps = take(0, xaT_done, c + 1)
                pe.wait_ge(xa_done, c + 1)
                for t in range(TPC):
                    mm = pe.transpose(ps[:, t * P:(t + 1) * P], XN[:, c * TPC + t, 0:H], ident)
                mm.then_inc(xa_turned, 1)

            def a_gram(c):
                ps = take(1, gram_sb, c + 1)
                tpb = TPC // BPC
                for b in range(BPC):
                    for t in range(tpb):
                        rows = XN[:, c * TPC + b * tpb + t, 0:H]
                        mm = pe.matmul(ps[:, b * P:(b + 1) * P], rows, rows, start=(t == 0), stop=(t == tpb - 1))
                mm.then_inc(gram_ps, 1)

            def a_gq(c):
                ps = take(0, gq_sb, c + 1)
                pe.wait_ge(gram_sb, c + 1)
                if c == 0:
                    pe.wait_ge(attn_in, 16)
                for b in range(BPC):
                    mm = pe.matmul(ps[:, b * P:(b + 1) * P], gram[:, c % 2, b, :], wqT, start=True, stop=True)
                mm.then_inc(gq_ps, 1)

            def a_kq(c):
                ps = take(1, kq_read, c + 1)
                pe.wait_ge(gq_sb, c + 1)
                pe.matmul(ps[:, 0:BPC * P], wkT, gq[:, c % 2].rearrange("p b q -> p (b q)"), start=True, stop=True)\
                    .then_inc(kq_ps, 1)

            def a_pv(c):
                ps = take(0, pv_sb, c + 1)
                pe.wait_ge(zb_done, c + 1)
                for b in range(BPC):
                    mm = pe.matmul(ps[:, b * P:(b + 1) * P], zb[:, c % 2, b, :], wv, start=True, stop=True)
                mm.then_inc(pv_ps, 1)

            def a_mix(c):
                ps = take(1, mix_sb, c + 1)
                pe.wait_ge(pv_sb, c + 1)
                for b in range(BPC):
                    mm = pe.matmul(ps[:, b * P:(b + 1) * P], pv[:, c % 2, b, :], woT, start=True, stop=True)
                mm.then_inc(mix_ps, 1)

            def a_out(c):
                ps = take(0, attn_added, c + 1)
                pe.wait_ge(mix_sb, c + 1)
                for t in range(TPC):
                    mm = pe.matmul(ps[:, t * P:(t + 1) * P], xaT[:, c % XA_RING, t * P:(t + 1) * P],
                                   mix[:, c % 2, t * BPC // TPC, :], start=True, stop=True)
                mm.then_inc(attn_ps, 1)

            do = dict(transpose=transpose, route=route, rank=rank, gathered=gathered, out_turn=out_turn,
                      a_turn=a_turn, a_gram=a_gram, a_gq=a_gq, a_kq=a_kq, a_pv=a_pv, a_mix=a_mix, a_out=a_out)
            pe.wait_ge(const_in, 32)
            pe.wait_ge(bf_ready, 2)
            for n in range(-1, LAST + 1):
                if 0 <= n < NSLOT:
                    gate_up(n)
                if 2 <= n < NSLOT + 2:
                    down(n - 2)
                for name, arg in stages.get(n, ()):
                    if name in do:
                        do[name](arg)

        @block.scalar
        def _(act):
            act.dma_start(cst[:], consts).then_inc(const_in, 16)
            act.dma_start(wr[:], w_router).then_inc(const_in, 16)

            def silu(n):
                N = slots[n][4]
                act.wait_ge(gu_done, n + 1)
                if n >= 2:
                    act.wait_ge(hidden_done, n - 1)
                act.activation(S[:, n % 2, 0:N], psG[n % 2][:, 0:N], ACT.Silu).then_inc(silu_done, 1)

            def split(p):
                raw_ready(act, p)
                act.copy(wgu_hi[:, p * PIECE:(p + 1) * PIECE], raw[:, p % RAW_RING, :]).then_inc(hi_split, 1)

            def transpose(q):
                act.wait_ge(xT_turned, q + 1)
                act.copy(xT_hi[:, q % CHUNKS, :], psM[0][:]).then_inc(xT_hi_done, 1)

            def route(q):
                act.wait_ge(gap_done, q + 1)
                act.activation(tanh_gap[:, q % 2, :], gap[:, q % 2, :], ACT.Tanh, scale=0.5).then_inc(tanh_done, 1)

            def gathered(le):
                g = gidx(*le)
                act.wait_ge(xg_turned, g + 1)
                act.copy(xgT_hi[:, g % 2, :], psM[0][:, 0:CAP]).then_inc(xg_hi_done, 1)

            def out_copy(u):
                N = slots[last_slot[u]][4]
                act.wait_ge(down_done, last_slot[u] + 1)
                if u:
                    act.wait_ge(out_turned, u)
                act.copy(oT[:, 0:N], psD[u % 2][:, 0:N]).then_inc(out_copied, 1)

            def a_turn(c):
                act.wait_ge(xa_turned, c + 1)
                if c >= XA_RING:
                    act.wait_ge(attn_ps, c - XA_RING + 1)
                act.copy(xaT[:, c % XA_RING, :], psM[0][:]).then_inc(xaT_done, 1)

            def small(c, ps_done, bank, dst, done, used):
                act.wait_ge(ps_done, c + 1)
                if c >= 2:
                    act.wait_ge(used, c - 1)
                act.copy(dst[:, c % 2].rearrange("p b q -> p (b q)"), psM[bank][:, 0:BPC * P])\
                    .then_inc(done, 1)

            def a_gram(c):
                small(c, gram_ps, 1, gram, gram_sb, gq_ps)

            def a_gq(c):
                small(c, gq_ps, 0, gq, gq_sb, kq_ps)

            def a_soft(c):
                act.wait_ge(zs_done, c + 1)
                act.activation(zt[:, c % 2], zs[:, c % 2], ACT.Tanh, scale=0.5 * SCALE).then_inc(zt_done, 1)

            def a_pv(c):
                small(c, pv_ps, 0, pv, pv_sb, mix_ps)

            def a_mix(c):
                small(c, mix_ps, 1, mix, mix_sb, attn_ps)

            do = dict(split=split, transpose=transpose, route=route, gathered=gathered, out_copy=out_copy, a_turn=a_turn,
                      a_gram=a_gram, a_gq=a_gq, a_soft=a_soft, a_pv=a_pv, a_mix=a_mix)
            for n in range(-1, LAST + 1):
                if 0 <= n < NSLOT:
                    silu(n)
                for name, arg in stages.get(n, ()):
                    if name in do:
                        do[name](arg)

        @block.vector
        def _(dve):
            steps = [0]

            def then(ins):
                steps[0] += 1
                ins.then_inc(dve_step, 1)
                dve.wait_ge(dve_step, steps[0])

            def hidden(n):
                N = slots[n][4]
                dve.wait_ge(silu_done, n + 1)
                if n >= H_RING:
                    dve.wait_ge(down_done, n - H_RING + 1)
                dve.tensor_tensor(Hd[:, n % H_RING, 0:N], S[:, n % 2, 0:N], psU[n % 2][:, 0:N], ALU.mult)\
                    .then_inc(hidden_done, 1)

            def split(p):
                dve.wait_ge(hi_split, p + 1)
                cols = slice(p * PIECE, (p + 1) * PIECE)
                dve.tensor_tensor(wgu_lo[:, cols], raw[:, p % RAW_RING, :], wgu_hi[:, cols].bitcast(F32), ALU.subtract)\
                    .then_inc(lo_split, 1)

            def stats(k, c, done):
                for t in range(TPC):
                    ins = dve.bn_stats(stat[:, k, t, :], X[:, c * TPC + t, :])
                then(ins)
                for t in range(TPC):
                    ins = dve.bn_aggr(mv[:, k, t, :], stat[:, k, t, :])
                then(ins)
                then(dve.tensor_scalar(pow_in[:, k, 0, :], mv[:, k, :, 1], LN_EPS, None, ALU.add))
                then(dve.reciprocal(var_eps[:, k, :], pow_in[:, k, 0, :]))
                then(dve.tensor_tensor(var_eps[:, k, :], var_eps[:, k, :], mv[:, k, :, 1], ALU.mult))
                dve.tensor_scalar(pow_in[:, k, 1, :], var_eps[:, k, :], RMS_EPS, None, ALU.add).then_inc(done, 1)

            def normalise(k, c, done):
                for t in range(TPC):
                    ins = dve.tensor_scalar(XN[:, c * TPC + t, 0:H], X[:, c * TPC + t, :], mv[:, k, t, 0:1],
                                            pow_out[:, k, 0, t:t + 1], ALU.subtract, ALU.mult)
                ins.then_inc(done, 1)

            def ln(q):
                if q < CHUNKS:
                    dve.wait_ge(x_in[q], 16)
                stats(q, q % CHUNKS, ln_stats)

            def apply(q):
                dve.wait_ge(ln_pow, q + 1)
                if q >= CHUNKS:
                    dve.wait_ge(gram_ps, q - CHUNKS + 1)
                normalise(q, q % CHUNKS, xn_done)

            def transpose(q):
                dve.wait_ge(xT_hi_done, q + 1)
                c = q % CHUNKS
                dve.tensor_tensor(xT_lo[:, c, :], psM[0][:], xT_hi[:, c, :].bitcast(F32), ALU.subtract)\
                    .then_inc(xT_lo_done, 1)

            def route(q):
                r = q % 2
                if q >= 2:
                    dve.wait_ge(ranks_done, q - 1)
                dve.wait_ge(logits_done, q + 1)
                ins = dve.tensor_tensor(logit[:], psM[1][:, 0:TPC * E].rearrange("p (t e) -> p t e", e=E),
                                        pow_out[:, q, 1, :].unsqueeze(2).to_broadcast([P, TPC, E]), ALU.mult)
                ins.then_inc(logits_read, 1)
                dve.wait_ge(logits_read, q + 1)
                for t in range(TPC):
                    ins = dve.max(top_v[:, r, t, :], logit[:, t, :])
                then(ins)
                dve.tensor_tensor(gap[:, r, :], top_v[:, r, :, 0], top_v[:, r, :, 1], ALU.subtract).then_inc(gap_done, 1)
                for t in range(TPC):
                    ins = dve.max_index(top_i[:, r, t, :], top_v[:, r, t, :], logit[:, t, :])
                then(ins)
                then(dve.tensor_tensor(choice[:, r], iota_e[:].unsqueeze(1).unsqueeze(1).to_broadcast([P, TOP, TPC, E]),
                                       top_i[:, r, :, 0:TOP].rearrange("p t k -> p k t").unsqueeze(3)
                                       .to_broadcast([P, TOP, TPC, E]), ALU.is_equal))
                ins = dve.tensor_tensor(mask[:, r], choice[:, r, 0], choice[:, r, 1], ALU.add)
                ins.then_inc(masks_done, 1)
                if q % CHUNKS < CHUNKS - 1:
                    dve.wait_ge(masks_done, q + 1)
                    then(dve.tensor_reduce(seen_c[:], mask[:, r].rearrange("p t e -> p e t"), AX.X, ALU.add))
                    if q % CHUNKS == 0:
                        then(dve.tensor_copy(seen[:, 1 - r], seen_c[:]))
                    else:
                        then(dve.tensor_tensor(seen[:, 1 - r], seen[:, r], seen_c[:], ALU.add))

            def rank(q):
                r, c = q % 2, q % CHUNKS
                dve.wait_ge(tanh_done, q + 1)
                rows = XN[:, tiles_of(c), :]
                dve.tensor_copy(rows[:, :, COL_E0], top_i[:, r, :, 0])
                dve.tensor_scalar(rows[:, :, COL_W1], tanh_gap[:, r, :], -0.25, 0.25, ALU.mult, ALU.add)
                then(dve.tensor_scalar(rows[:, :, COL_DW], tanh_gap[:, r, :], 0.5, None, ALU.mult))
                dve.wait_ge(ranks_done, q + 1)
                ps = psM[1][:, 0:TPC * E].rearrange("p (t e) -> p t e", e=E)
                dve.tensor_scalar(late[:], ps, float(CAP), float(FAR), ALU.is_ge, ALU.mult)
                ins = dve.tensor_tensor(place[:], ps, slot_base[:].unsqueeze(1).to_broadcast([P, TPC, E]), ALU.add)
                ins.then_inc(ranks_read, 1)
                dve.wait_ge(ranks_read, q + 1)
                then(dve.tensor_tensor(place[:], place[:], late[:], ALU.add))
                then(dve.tensor_tensor(picked[:], choice[:, r], place[:].unsqueeze(1).to_broadcast([P, TOP, TPC, E]),
                                       ALU.mult))
                then(dve.tensor_reduce(place_f[:], picked[:], AX.X, ALU.add))
                dve.tensor_scalar(place_u[:, q], place_f[:], float(E * CAP), None, ALU.min).then_inc(places_done, 1)

            def gathered(le):
                l, e = le
                g = gidx(l, e)
                r = g % XG_RING
                dve.wait_ge(xg_hi_done, g + 1)
                dve.tensor_tensor(xgT_lo[:, g % 2, :], psM[0][:, 0:CAP], xgT_hi[:, g % 2, :].bitcast(F32), ALU.subtract)\
                    .then_inc(xg_lo_done, 1)
                then(dve.tensor_scalar(wsl[:, r, :], xg[:, r, :, COL_E0], float(e), None, ALU.is_equal))
                then(dve.tensor_tensor(wsl[:, r, :], wsl[:, r, :], xg[:, r, :, COL_DW], ALU.mult))
                then(dve.tensor_tensor(wsl[:, r, :], wsl[:, r, :], xg[:, r, :, COL_W1], ALU.add))

            def out_turn(u):
                kind, l, i = units[u]
                dve.wait_ge(out_turned, u + 1)
                if kind == SHARED:
                    rows = X[:, tiles_of(i), :].rearrange("p t h -> p (t h)")
                    ins = dve.scalar_tensor_tensor(out=rows, in0=psM[1][:], scalar=0.5, in1=rows, op0=ALU.mult, op1=ALU.add)
                    ins.then_inc(out_read, 1)
                    dve.wait_ge(out_read, u + 1)
                else:
                    g = gidx(l, i)
                    if g >= 2:
                        dve.wait_ge(added, 16 * NB * (g - 1))
                    for j, (r0, n) in enumerate(BLOCKS):
                        ins = dve.tensor_scalar(yw[0:n, g % 2, j, :], psM[1][0:n, j * P:(j + 1) * P],
                                                wsl[0:n, g % XG_RING, j:j + 1], None, ALU.mult)
                    ins.then_inc(out_read, 1)

            def add_sums(k, c):
                dve.wait_ge(sums_in[k % 2], 16 * (k // 2 + 1))
                ins = dve.tensor_tensor(X[:, tiles_of(c), :], X[:, tiles_of(c), :], sums[:, k % 2], ALU.add)
                ins.then_inc(combined, 1)
                dve.wait_ge(combined, k + 1)

            def combine(c):
                add_sums(c, c)
                stats(LAYERS * CHUNKS + c, c, an_stats)

            def finish(c):
                add_sums(CHUNKS + c, c)

            def a_apply(c):
                dve.wait_ge(an_pow, c + 1)
                if c == 0:
                    dve.wait_ge(dispatched[0], 16 * TOP * TILES)
                normalise(LAYERS * CHUNKS + c, c, xa_done)

            def a_kq(c):
                dve.wait_ge(kq_ps, c + 1)
                ins = dve.tensor_tensor(kq[:], psM[1][:, 0:BPC * P].rearrange("p (b q) -> p b q", b=BPC),
                                        block_mask.unsqueeze(1).to_broadcast([P, BPC, P]), ALU.mult)
                ins.then_inc(kq_read, 1)
                dve.wait_ge(kq_read, c + 1)
                then(dve.tensor_reduce(zc[:], kq[:].rearrange("p b (g j) -> p b j g", j=HEAD), AX.X, ALU.add))
                then(dve.tensor_reduce(zmax[:], zc[:], AX.X, ALU.max))
                dve.tensor_tensor(zs[:, c % 2], zc[:], zmax[:].unsqueeze(2).to_broadcast([P, BPC, HEAD]), ALU.subtract)\
                    .then_inc(zs_done, 1)

            def a_soft(c):
                dve.wait_ge(zt_done, c + 1)
                dve.tensor_scalar(znum[:], zt[:, c % 2], 1.0, None, ALU.add)
                then(dve.tensor_scalar(zden[:], zt[:, c % 2], -1.0, 1.0, ALU.mult, ALU.add))
                then(dve.reciprocal(zden[:], zden[:]))
                then(dve.tensor_tensor(znum[:], znum[:], zden[:], ALU.mult))
                then(dve.tensor_reduce(zsum[:], znum[:], AX.X, ALU.add))
                then(dve.reciprocal(zsum[:], zsum[:]))
                then(dve.tensor_tensor(znum[:], znum[:], zsum[:].unsqueeze(2).to_broadcast([P, BPC, HEAD]), ALU.mult))
                if c >= 2:
                    dve.wait_ge(pv_ps, c - 1)
                for b in range(BPC):
                    ins = dve.tensor_tensor(zb[:, c % 2, b, :].rearrange("p (g j) -> p g j", j=HEAD),
                                            block_mask.rearrange("p (g j) -> p g j", j=HEAD),
                                            znum[:, b, :].unsqueeze(1).to_broadcast([P, P // HEAD, HEAD]), ALU.mult)
                ins.then_inc(zb_done, 1)

            def a_out(c):
                dve.wait_ge(attn_ps, c + 1)
                rows = X[:, tiles_of(c), :].rearrange("p t h -> p (t h)")
                ins = dve.tensor_tensor(rows, psM[0][:], rows, ALU.add)
                ins.then_inc(attn_added, 1)
                dve.wait_ge(attn_added, c + 1)

            do = dict(split=split, ln=ln, apply=apply, transpose=transpose, route=route, rank=rank, gathered=gathered,
                      out_turn=out_turn, combine=combine, finish=finish, a_apply=a_apply, a_kq=a_kq, a_soft=a_soft,
                      a_out=a_out)
            dve.memset(zeros[:], 0.0)
            dve.memset(xg[:], 0.0).then_inc(dve_const, 1)
            dve.wait_ge(dve_const, 1)
            dve.wait_ge(const_in, 32)
            dve.tensor_copy(tri[:], cst[:, 2 * P:3 * P]).then_inc(bf_ready, 1)
            dve.memset(ones[:], 1.0).then_inc(bf_ready, 1)
            dve.wait_ge(pool_const, 2)
            for n in range(-1, LAST + 1):
                if 0 <= n < NSLOT:
                    hidden(n)
                for name, arg in stages.get(n, ()):
                    if name in do:
                        do[name](arg)

        @block.gpsimd
        def _(pool):
            steps = [0]

            def then(ins):
                steps[0] += 1
                ins.then_inc(pool_step, 1)
                pool.wait_ge(pool_step, steps[0])

            then(pool.memset(mhalf[:], -0.5))
            then(pool.memset(init_row[:], 0.0))
            pool.iota(init_row[:, COL_ID:COL_ID + 1].bitcast(U32), pattern=[[0, 1]], base=T, channel_multiplier=1)\
                .then_inc(pool_const, 1)
            then(pool.iota(XN[:, :, COL_ID].bitcast(U32), pattern=[[P, TILES]], base=0, channel_multiplier=1))
            then(pool.iota(iota_e[:], pattern=[[1, E]], base=0, channel_multiplier=0, allow_small_or_imprecise_dtypes=True))
            then(pool.iota(slot_base[:], pattern=[[CAP, E]], base=0, channel_multiplier=0, allow_small_or_imprecise_dtypes=True))
            pool.memset(wsl[:], 0.0).then_inc(pool_const, 1)

            def powers(k, ready, need, done):
                pool.wait_ge(ready, need)
                pool.tensor_tensor(pow_out[:, k], pow_in[:, k], mhalf[:], ALU.pow).then_inc(done, 1)

            def ffn_pow(q):
                powers(q, ln_stats, q + 1, ln_pow)

            def attn_pow(c):
                powers(LAYERS * CHUNKS + c, an_stats, c + 1, an_pow)

            def dispatch(q, tiles=range(TPC)):
                l, c = q // CHUNKS, q % CHUNKS
                pool.wait_ge(places_done, q + 1)
                if q == 0:
                    pool.wait_ge(init_done, 16 * LAYERS * (CHUNKS + 2))
                for t in tiles:
                    for k in range(TOP):
                        pool.indirect_dma_start(
                            out=rows_dram[l], out_offset=bass.IndirectOffsetOnAxis(ap=place_u[:, q, k, t:t + 1], axis=0),
                            in_=XN[:, c * TPC + t, :], in_offset=None, bounds_check=E * CAP - 1, oob_is_err=False,
                        ).then_inc(dispatched[l], 16)

            def add_outputs(l, e):
                g = gidx(l, e)
                pool.wait_ge(out_read, unit_of[(EXPERT, l, e)] + 1)
                if g:
                    pool.wait_ge(added, 16 * NB * g)
                for j, (r0, n) in enumerate(BLOCKS):
                    pool.indirect_dma_start(
                        out=sums_dram[l],
                        out_offset=bass.IndirectOffsetOnAxis(ap=xg[0:n, g % XG_RING, j, COL_ID:COL_ID + 1].bitcast(U32), axis=0),
                        in_=yw[0:n, g % 2, j, :], in_offset=None, compute_op=ALU.add,
                    ).then_inc(added, 16)

            half = range(TPC // 2), range(TPC // 2, TPC)
            for q in range(CHUNKS):
                ffn_pow(q)
            for q in range(CHUNKS):
                dispatch(q)
            for e in range(E):
                add_outputs(0, e)
            attn_pow(0)
            attn_pow(1)
            attn_pow(2)
            ffn_pow(4)
            ffn_pow(5)
            dispatch(4, half[0])
            attn_pow(3)
            ffn_pow(6)
            dispatch(4, half[1])
            dispatch(5)
            dispatch(6, half[0])
            ffn_pow(7)
            dispatch(6, half[1])
            dispatch(7)
            for e in range(E):
                add_outputs(1, e)


def kernel(**inputs):
    import numpy as np
    import concourse.bacc as bacc
    from concourse import mybir as _mybir
    from concourse.bass_utils import run_bass_kernel_spmd

    a = {k: np.asarray(v) for k, v in inputs.items()}
    x = a["L0_attn_x"]
    B, S, H = x.shape
    T = B * S
    E = a["L0_ffn_rg"].shape[0]

    def hidden_last(w):
        w = w.reshape(-1, H, w.shape[-1] // P, P)
        return w.transpose(1, 0, 2, 3).reshape(H, -1, P)

    def hidden_first(w):
        return w.reshape(-1, P, H).transpose(1, 0, 2)

    gate = np.concatenate([hidden_last(a["L0_ffn_sg"]), hidden_last(a["L0_ffn_rg"])], axis=1)
    up = np.concatenate([hidden_last(a["L0_ffn_su"]), hidden_last(a["L0_ffn_ru"])], axis=1)
    down = np.concatenate([hidden_first(a["L0_ffn_sd"]), hidden_first(a["L0_ffn_rd"])], axis=1)
    r = np.arange(P)
    consts = np.concatenate([r[:, None] == r, r[:, None] // 8 == r // 8, r[:, None] < r], axis=1)
    arrays = {
        "x": x.reshape(T, H),
        "w_gate_up": np.stack([gate, up], axis=2).reshape(H, -1),
        "w_down": down.reshape(P, -1),
        "w_attn": np.concatenate([a["L0_attn_Wq"].T, a["L0_attn_Wk"].T, a["L0_attn_Wv"], a["L0_attn_Wo"].T], axis=1),
        "w_router": a["L0_ffn_router_w"].T,
        "consts": consts.astype(np.float32),
    }
    arrays = {k: np.ascontiguousarray(v) for k, v in arrays.items()}
    nc = bacc.Bacc("TRN2", target_bir_lowering=False, num_devices=1)
    args = [nc.dram_tensor(k, v.shape, _mybir.dt.from_np(v.dtype), kind="ExternalInput").ap() for k, v in arrays.items()]
    out = nc.dram_tensor("out", (T, H), _mybir.dt.float32, kind="ExternalOutput").ap()
    macaron_block_kernel(nc, *args, out)
    res = run_bass_kernel_spmd(nc, [arrays], core_ids=[0])
    return res.results[0]["out"].reshape(B, S, H)
```

```python
from contextlib import ExitStack

import concourse.bass as bass
from concourse import mybir

ALU = mybir.AluOpType
ACT = mybir.ActivationFunctionType
AX = mybir.AxisListType
F32 = mybir.dt.float32
F32R = mybir.dt.float32r
BF16 = mybir.dt.bfloat16
U32 = mybir.dt.uint32

P = 128


def macaron_block_kernel(nc, x, w_gate_up, w_down, w_attn, w_router, consts, out):
    T, H = x.shape
    LAYERS = 2
    E = w_router.shape[1]
    HT = w_down.shape[1] // P
    HT_EXPERT = 4 * H // P
    HT_SHARED = HT - E * HT_EXPERT
    CAP = max(int(1.25 * T / E), 1)
    TILES = T // P
    TPC = 4
    CHUNKS = TILES // TPC
    C = TPC * P
    SEQ = 2 * P
    BPC = C // SEQ
    HEAD = 8
    TOP = 2
    BLOCKS = [(j * P, min(P, CAP - j * P)) for j in range((CAP + P - 1) // P)]
    NB = len(BLOCKS)
    ROW = H + 4
    COL_ID, COL_E0, COL_W1, COL_DW = H, H + 1, H + 2, H + 3
    FAR = 4096
    LN_EPS = 1e-5
    RMS_EPS = 1.1920928955078125e-07
    SCALE = float(HEAD) ** -0.5
    HPP = 2
    PIECES = HT // HPP
    PIECE = HPP * 2 * P
    RAW_RING, XG_RING, H_RING, XA_RING = 4, 6, 3, 3

    SHARED, EXPERT = "shared", "expert"
    order = [[(SHARED, 0), (SHARED, 1)] + [(EXPERT, e) for e in range(E)] + [(SHARED, 2), (SHARED, 3)],
             [(SHARED, 0), (SHARED, 1), (SHARED, 2)] + [(EXPERT, e) for e in range(E)] + [(SHARED, 3)]]
    units, slots, first_slot, last_slot = [], [], {}, {}
    for l in range(LAYERS):
        for kind, i in order[l]:
            u = len(units)
            units.append((kind, l, i))
            tiles = HT_SHARED if kind == SHARED else HT_EXPERT
            base = 0 if kind == SHARED else HT_SHARED + i * HT_EXPERT
            first_slot[u] = len(slots)
            for k in range(tiles):
                slots.append((u, k, tiles, base + k, C if kind == SHARED else CAP))
            last_slot[u] = len(slots) - 1
    unit_of = {v: u for u, v in enumerate(units)}
    NSLOT = len(slots)

    stages = {}

    def at(half_slot, name, arg):
        stages.setdefault(half_slot, []).append((name, arg))

    for name, arg in (("ln", 0), ("ln", 1), ("apply", 0), ("ln", 2), ("transpose", 0), ("split", 0), ("split", 1)):
        at(-1, name, arg)
    for slot, half, name, arg in (
            (0, 1, "route", 0), (0, 1, "apply", 1), (1, 0, "split", 2), (1, 1, "rank", 0), (1, 1, "transpose", 1),
            (2, 1, "ln", 3), (2, 1, "apply", 2), (3, 0, "split", 3), (3, 1, "route", 1), (3, 1, "transpose", 2),
            (4, 1, "rank", 1), (5, 1, "route", 2), (5, 1, "apply", 3), (6, 1, "rank", 2), (6, 1, "transpose", 3),
            (8, 1, "route", 3), (9, 1, "rank", 3)):
        at(2 * slot + half, name, arg)
    for p in range(4, PIECES):
        at(2 * (p + 6) if p < 10 else 2 * (p + 5), "split", p)
    for u, (kind, l, i) in enumerate(units):
        at(2 * (last_slot[u] + 2) + 1, "out_copy", u)
        at(2 * (last_slot[u] + 3), "out_turn", u)
        if kind == EXPERT:
            at(2 * (first_slot[u] - (1 if i == 0 else 2)) + 1, "gathered", (l, i))
    groups = ((0, 1), (2,), (3,))
    for g, s in enumerate((108, 126, 134)):
        for d, name in ((5, "a_gram"), (6, "a_gq"), (7, "a_kq"), (9, "a_soft"), (10, "a_pv"), (11, "a_mix")):
            at(s + d + len(groups[g]) - 1, name, g)
        for j, c in enumerate(groups[g]):
            for d, name in ((0, "combine"), (3, "a_apply"), (4, "a_turn")):
                at(s + d + j, name, c)
            s2 = s + j + len(groups[g]) - 1
            at(s2 + 12, "a_out", c)
            for d, name in ((12, "ln"), (15, "apply"), (16, "transpose"), (20 + 2 * j, "route"), (22 + 2 * j, "rank")):
                at(s2 + d, name, CHUNKS + c)
    for c, s in enumerate((125, 126, 127, 130)):
        at(2 * s + 1, "finish", c)
    LAST = max(stages) // 2
    group_of = {c: g for g, cs in enumerate(groups) for c in cs}

    with ExitStack() as ctx:
        def sb(name, shape, dt=F32):
            return ctx.enter_context(nc.sbuf_tensor(name, shape, dt))

        def pb(name, shape):
            return ctx.enter_context(nc.psum_tensor(name, shape, F32))

        def sem(name):
            return ctx.enter_context(nc.semaphore(name))

        rows_dram = [nc.dram_tensor(f"rows_{l}", [E * CAP, ROW], F32, kind="Internal").ap() for l in range(LAYERS)]
        sums_dram = [nc.dram_tensor(f"sums_{l}", [T + P, H], F32, kind="Internal").ap() for l in range(LAYERS)]

        cst = sb("cst", [P, 3 * P])
        ident, block_mask = cst[:, 0:P], cst[:, P:2 * P]
        wa = sb("wa", [P, 4 * P])
        wqT, wkT, wv, woT = (wa[:, i * P:(i + 1) * P] for i in range(4))
        wr = sb("wr", [P, E])
        wr_hi = sb("wr_hi", [P, E], F32R)
        wr_lo = sb("wr_lo", [P, E], F32R)
        tri = sb("tri", [P, P], BF16)
        ones = sb("ones", [P, P], BF16)
        iota_e = sb("iota_e", [P, E])
        slot_base = sb("slot_base", [P, E])
        mhalf = sb("mhalf", [P, TPC])
        warm = sb("warm", [P, TPC])
        init_row = sb("init_row", [P, ROW])
        zeros = sb("zeros", [P, C])

        raw = sb("raw", [P, RAW_RING, PIECE])
        wgu_hi = sb("wgu_hi", [P, HT * 2 * P], F32R)
        wgu_lo = sb("wgu_lo", [P, HT * 2 * P], F32R)
        wd = sb("wd", [P, HT * P])

        X = sb("X", [P, TILES, H])
        XN = sb("XN", [P, TILES, ROW])
        xT_hi = sb("xT_hi", [P, CHUNKS, C], F32R)
        xT_lo = sb("xT_lo", [P, CHUNKS, C], F32R)
        S = sb("S", [P, 2, C])
        Hd = sb("Hd", [P, H_RING, C])
        oT = sb("oT", [P, C])
        xg = sb("xg", [P, XG_RING, NB, ROW])
        xgT_hi = sb("xgT_hi", [P, 2, CAP], F32R)
        xgT_lo = sb("xgT_lo", [P, 2, CAP], F32R)
        wsl = sb("wsl", [P, XG_RING, NB])
        yw = sb("yw", [P, 2, NB, H])
        sums = sb("sums", [P, 2, TPC, H])

        NLN = (LAYERS + 1) * CHUNKS
        stat = sb("stat", [P, NLN, TPC, 6])
        mv = sb("mv", [P, NLN, TPC, 2])
        var_eps = sb("var_eps", [P, NLN, TPC])
        rstd = sb("rstd", [P, NLN, TPC])
        neg_mean = sb("neg_mean", [P, NLN, TPC])
        shift = sb("shift", [P, NLN, TPC])
        msq = sb("msq", [P, NLN, TPC])
        rrms = sb("rrms", [P, LAYERS * CHUNKS, TPC])
        logit = sb("logit", [P, TPC, E])
        top_v = sb("top_v", [P, 2, TPC, 8])
        top_i = sb("top_i", [P, 2, TPC, 8], U32)
        choice = sb("choice", [P, 2, TOP, TPC, E])
        mask = sb("mask", [P, 2, TPC, E], BF16)
        seen = sb("seen", [P, 2, E], BF16)
        seen_c = sb("seen_c", [P, E])
        gap = sb("gap", [P, 2, TPC])
        tanh_gap = sb("tanh_gap", [P, 2, TPC])
        late = sb("late", [P, TPC, E])
        place = sb("place", [P, TPC, E])
        picked = sb("picked", [P, TOP, TPC, E])
        place_f = sb("place_f", [P, TOP, TPC])
        place_u = sb("place_u", [P, LAYERS * CHUNKS, TOP, TPC], U32)

        NBG = max(len(g) for g in groups) * BPC
        xaT = sb("xaT", [P, XA_RING, C])
        gram = sb("gram", [P, NBG, P])
        gq = sb("gq", [P, NBG, P])
        kq = sb("kq", [P, NBG, P])
        zc = sb("zc", [P, NBG, HEAD])
        zmax = sb("zmax", [P, NBG])
        zs = sb("zs", [P, NBG, HEAD])
        zt = sb("zt", [P, NBG, HEAD])
        znum = sb("znum", [P, NBG, HEAD])
        zden = sb("zden", [P, NBG, HEAD])
        zsum = sb("zsum", [P, NBG])
        zb = sb("zb", [P, NBG, P])
        pv = sb("pv", [P, NBG, P])
        mix = sb("mix", [P, NBG, P])

        psG = [pb(f"psG{i}", [P, C]) for i in range(2)]
        psU = [pb(f"psU{i}", [P, C]) for i in range(2)]
        psD = [pb(f"psD{i}", [P, C]) for i in range(2)]
        psM = [pb(f"psM{i}", [P, C]) for i in range(2)]

        const_in = sem("const_in")
        x_in = [sem(f"x_in{c}") for c in range(CHUNKS)]
        attn_in = sem("attn_in")
        down_in = [sem(f"down_in{i}") for i in range(2)]
        raw_in = [sem(f"raw_in{i}") for i in range(RAW_RING)]
        hi_split, lo_split = sem("hi_split"), sem("lo_split")
        bf_ready = sem("bf_ready")
        pool_const, dve_const = sem("pool_const"), sem("dve_const")
        rows_init = [sem(f"rows_init{l}") for l in range(LAYERS)]
        sums_init = [sem(f"sums_init{l}") for l in range(LAYERS)]
        wr_hi_done, wr_done = sem("wr_hi_done"), sem("wr_done")
        rms_pow = sem("rms_pow")
        gu_done, silu_done, hidden_done, down_done = sem("gu_done"), sem("silu_done"), sem("hidden_done"), sem("down_done")
        out_copied, out_turned = sem("out_copied"), sem("out_turned")
        out_read, logits_read, ranks_read = sem("out_read"), sem("logits_read"), sem("ranks_read")
        kq_read, attn_added = sem("kq_read"), sem("attn_added")
        dve_step, pool_step = sem("dve_step"), sem("pool_step")
        ln_stats, ln_pow, xn_done = sem("ln_stats"), sem("ln_pow"), sem("xn_done")
        an_stats, an_pow, xa_done = sem("an_stats"), sem("an_pow"), sem("xa_done")
        xT_turned, xT_hi_done, xT_lo_done = sem("xT_turned"), sem("xT_hi_done"), sem("xT_lo_done")
        logits_done, masks_done, gap_done, tanh_done = sem("logits_done"), sem("masks_done"), sem("gap_done"), sem("tanh_done")
        ranks_done, places_done = sem("ranks_done"), sem("places_done")
        dispatched = [sem(f"dispatched{l}") for l in range(LAYERS)]
        rows_in = [sem(f"rows_in{i}") for i in range(XG_RING)]
        xg_turned, xg_hi_done, xg_lo_done = sem("xg_turned"), sem("xg_hi_done"), sem("xg_lo_done")
        added = sem("added")
        sums_in = [sem(f"sums_in{i}") for i in range(2)]
        combined = sem("combined")
        xa_turned, xaT_done = sem("xa_turned"), sem("xaT_done")
        gram_ps, gram_sb, gq_ps, gq_sb, kq_ps = sem("gram_ps"), sem("gram_sb"), sem("gq_ps"), sem("gq_sb"), sem("kq_ps")
        zs_done, zt_done, zb_done = sem("zs_done"), sem("zt_done"), sem("zb_done")
        pv_ps, pv_sb, mix_ps, mix_sb, attn_ps = sem("pv_ps"), sem("pv_sb"), sem("mix_ps"), sem("mix_sb"), sem("attn_ps")
        stored = sem("stored")

        x_t = x.rearrange("(t p) h -> p t h", p=P)
        out_t = out.rearrange("(t p) h -> p t h", p=P)

        def tiles_of(c):
            return slice(c * TPC, (c + 1) * TPC)

        def gidx(l, e):
            return l * E + e

        def raw_ready(eng, p):
            eng.wait_ge(raw_in[p % RAW_RING], 16 * (p // RAW_RING + 1))

        block = ctx.enter_context(nc.Block())

        @block.sync
        def _(sp):
            def piece(p):
                if p >= RAW_RING:
                    sp.wait_ge(lo_split, p - RAW_RING + 1)
                sp.dma_start(raw[:, p % RAW_RING, :], w_gate_up[:, p * PIECE:(p + 1) * PIECE])\
                    .then_inc(raw_in[p % RAW_RING], 16)

            def load_x(c):
                sp.dma_start(X[:, tiles_of(c), :], x_t[:, tiles_of(c), :]).then_inc(x_in[c], 16)

            def init_rows(l):
                sp.dma_start(rows_dram[l].rearrange("(i p) c -> p i c", p=P),
                             init_row[:].unsqueeze(1).to_broadcast([P, E * CAP // P, ROW])).then_inc(rows_init[l], 16)

            def init_sums(l):
                for c in range(CHUNKS):
                    sp.dma_start(sums_dram[l][c * C:(c + 1) * C, :].rearrange("(p t) h -> p (t h)", p=P), zeros[:])\
                        .then_inc(sums_init[l], 16)
                sp.dma_start(sums_dram[l][T:T + P, :], zeros[:, 0:H]).then_inc(sums_init[l], 16)

            load_x(0)
            piece(0)
            load_x(1)
            piece(1)
            load_x(2)
            sp.dma_start(wd[:, 0:HT_SHARED * P], w_down[:, 0:HT_SHARED * P]).then_inc(down_in[0], 16)
            load_x(3)
            piece(2)
            piece(3)
            sp.wait_ge(pool_const, 2)
            init_rows(0)
            for p in range(4, 8):
                piece(p)
            sp.dma_start(wd[:, HT_SHARED * P:], w_down[:, HT_SHARED * P:]).then_inc(down_in[1], 16)
            sp.wait_ge(dve_const, 1)
            init_sums(0)
            for p in range(8, 12):
                piece(p)
            sp.dma_start(wa[:], w_attn).then_inc(attn_in, 16)
            for p in range(12, PIECES - 6):
                piece(p)
            init_rows(1)
            init_sums(1)
            for l in range(LAYERS):
                for e in range(E):
                    g = gidx(l, e)
                    if l == 0 and 2 <= e <= 4:
                        for p in range(PIECES - 10 + 2 * e, PIECES - 8 + 2 * e):
                            piece(p)
                    if e == 0:
                        sp.wait_ge(dispatched[l], 16 * TOP * TILES)
                    if g >= XG_RING:
                        sp.wait_ge(added, 16 * NB * (g - XG_RING + 1))
                    full = CAP // P
                    sp.dma_start(xg[:, g % XG_RING, 0:full, :],
                                 rows_dram[l][e * CAP:e * CAP + full * P, :].rearrange("(j p) c -> p j c", p=P))\
                        .then_inc(rows_in[g % XG_RING], 16)
                    for r0, n in BLOCKS[full:]:
                        sp.dma_start(xg[0:n, g % XG_RING, full, :],
                                     rows_dram[l][e * CAP + r0:e * CAP + r0 + n, :]).then_inc(rows_in[g % XG_RING], 16)
                sp.wait_ge(added, 16 * NB * E * (l + 1))
                for c in range(CHUNKS):
                    k = l * CHUNKS + c
                    if k >= 2:
                        sp.wait_ge(combined, k - 1)
                    sp.dma_start(sums[:, k % 2, :, :],
                                 sums_dram[l][c * C:(c + 1) * C, :].rearrange("(t p) h -> p t h", p=P))\
                        .then_inc(sums_in[k % 2], 16)
            for c in range(CHUNKS):
                sp.wait_ge(combined, CHUNKS + c + 1)
                sp.dma_start(out_t[:, tiles_of(c), :], X[:, tiles_of(c), :]).then_inc(stored, 16)
            sp.wait_ge(stored, 16 * CHUNKS)

        @block.tensor
        def _(pe):
            reader = [None, None]

            def take(bank, *read):
                if reader[bank]:
                    pe.wait_ge(*reader[bank])
                reader[bank] = read
                return psM[bank]

            def gate_up(n):
                u, k, tiles, ht, N = slots[n]
                kind, l, i = units[u]
                if n >= 2:
                    pe.wait_ge(hidden_done, n - 1)
                if l == 0 and (kind == EXPERT or i == 0):
                    pe.wait_ge(lo_split, ht // HPP + 1)
                if k == 0:
                    if kind == SHARED:
                        pe.wait_ge(xT_lo_done, l * CHUNKS + i + 1)
                    else:
                        pe.wait_ge(xg_lo_done, gidx(l, i) + 1)
                if kind == SHARED:
                    hi, lo = xT_hi[:, i, :], xT_lo[:, i, :]
                else:
                    hi, lo = xgT_hi[:, gidx(l, i) % 2, :], xgT_lo[:, gidx(l, i) % 2, :]
                for half, ps in ((0, psG[n % 2]), (1, psU[n % 2])):
                    o = (2 * ht + half) * P
                    pe.matmul(ps[:, 0:N], wgu_hi[:, o:o + P], hi, start=True, stop=False)
                    pe.matmul(ps[:, 0:N], wgu_hi[:, o:o + P], lo, start=False, stop=False)
                    mm = pe.matmul(ps[:, 0:N], wgu_lo[:, o:o + P], hi, start=False, stop=True)
                mm.then_inc(gu_done, 1)

            def down(n):
                u, k, tiles, ht, N = slots[n]
                pe.wait_ge(hidden_done, n + 1)
                if k == 0 and u >= 2:
                    pe.wait_ge(out_copied, u - 1)
                if u == 0 and k == 0:
                    pe.wait_ge(down_in[0], 16)
                if units[u][0] == EXPERT and k == 0:
                    pe.wait_ge(down_in[1], 16)
                pe.matmul(psD[u % 2][:, 0:N], wd[:, ht * P:(ht + 1) * P], Hd[:, n % H_RING, 0:N],
                          start=(k == 0), stop=(k == tiles - 1)).then_inc(down_done, 1)

            def transpose(q):
                c = q % CHUNKS
                ps = take(0, xT_lo_done, q + 1)
                pe.wait_ge(xn_done, q + 1)
                for t in range(TPC):
                    mm = pe.transpose(ps[:, t * P:(t + 1) * P], XN[:, c * TPC + t, 0:H], ident)
                mm.then_inc(xT_turned, 1)

            def route(q):
                c = q % CHUNKS
                pe.wait_ge(xT_lo_done, q + 1)
                if q == 0:
                    pe.wait_ge(wr_done, 1)
                ps = take(1, logits_read, q + 1)
                for t in range(TPC):
                    o = slice(t * P, (t + 1) * P)
                    for j, (xs, ws) in enumerate(((xT_hi, wr_hi), (xT_hi, wr_lo), (xT_lo, wr_hi))):
                        mm = pe.matmul(ps[:, t * E:(t + 1) * E], xs[:, c, o], ws[:], start=(j == 0), stop=(j == 2))
                mm.then_inc(logits_done, 1)

            def rank(q):
                c = q % CHUNKS
                pe.wait_ge(masks_done, q + 1)
                ps = take(1, ranks_read, q + 1)
                m = mask[:, q % 2]
                mm = pe.matmul(ps[:, 0:TPC * E], tri[:], m.rearrange("p t e -> p (t e)"), start=True, stop=True)
                for d in range(1, TPC):
                    mm = pe.matmul(ps[:, d * E:TPC * E], ones[:], m[:, 0:TPC - d, :].rearrange("p t e -> p (t e)"),
                                   start=False, stop=True, skip_group_check=True)
                if c:
                    mm = pe.matmul(ps[:, 0:TPC * E], ones[:], seen[:, q % 2].unsqueeze(1).to_broadcast([P, TPC, E]),
                                   start=False, stop=True, skip_group_check=True)
                mm.then_inc(ranks_done, 1)

            def gathered(le):
                g = gidx(*le)
                ps = take(0, xg_lo_done, g + 1)
                pe.wait_ge(rows_in[g % XG_RING], 32 * (g // XG_RING + 1))
                for j, (r0, n) in enumerate(BLOCKS):
                    mm = pe.transpose(ps[:, r0:r0 + n], xg[0:n, g % XG_RING, j, 0:H], ident[0:n, 0:n])
                mm.then_inc(xg_turned, 1)

            def out_turn(u):
                kind, l, i = units[u]
                ps = take(1, out_read, u + 1)
                pe.wait_ge(out_copied, u + 1)
                if kind == SHARED:
                    for t in range(TPC):
                        mm = pe.transpose(ps[:, t * P:(t + 1) * P], oT[:, t * P:(t + 1) * P], ident)
                else:
                    for j, (r0, n) in enumerate(BLOCKS):
                        mm = pe.transpose(ps[0:n, j * P:(j + 1) * P], oT[:, r0:r0 + n], ident)
                mm.then_inc(out_turned, 1)

            def a_turn(c):
                ps = take(0, xaT_done, c + 1)
                pe.wait_ge(xa_done, c + 1)
                for t in range(TPC):
                    mm = pe.transpose(ps[:, t * P:(t + 1) * P], XN[:, c * TPC + t, 0:H], ident)
                mm.then_inc(xa_turned, 1)

            def a_gram(g):
                ps = take(1, gram_sb, g + 1)
                tpb = TPC // BPC
                for b in range(len(groups[g]) * BPC):
                    for t in range(tpb):
                        rows = XN[:, groups[g][0] * TPC + b * tpb + t, 0:H]
                        mm = pe.matmul(ps[:, b * P:(b + 1) * P], rows, rows, start=(t == 0), stop=(t == tpb - 1))
                mm.then_inc(gram_ps, 1)

            def a_gq(g):
                ps = take(0, gq_sb, g + 1)
                pe.wait_ge(gram_sb, g + 1)
                if g == 0:
                    pe.wait_ge(attn_in, 16)
                for b in range(len(groups[g]) * BPC):
                    mm = pe.matmul(ps[:, b * P:(b + 1) * P], gram[:, b, :], wqT, start=True, stop=True)
                mm.then_inc(gq_ps, 1)

            def a_kq(g):
                ps = take(1, kq_read, g + 1)
                pe.wait_ge(gq_sb, g + 1)
                nb = len(groups[g]) * BPC
                pe.matmul(ps[:, 0:nb * P], wkT, gq[:, 0:nb].rearrange("p b q -> p (b q)"), start=True, stop=True)\
                    .then_inc(kq_ps, 1)

            def a_pv(g):
                ps = take(0, pv_sb, g + 1)
                pe.wait_ge(zb_done, g + 1)
                for b in range(len(groups[g]) * BPC):
                    mm = pe.matmul(ps[:, b * P:(b + 1) * P], zb[:, b, :], wv, start=True, stop=True)
                mm.then_inc(pv_ps, 1)

            def a_mix(g):
                ps = take(1, mix_sb, g + 1)
                pe.wait_ge(pv_sb, g + 1)
                for b in range(len(groups[g]) * BPC):
                    mm = pe.matmul(ps[:, b * P:(b + 1) * P], pv[:, b, :], woT, start=True, stop=True)
                mm.then_inc(mix_ps, 1)

            def a_out(c):
                ps = take(0, attn_added, c + 1)
                pe.wait_ge(mix_sb, group_of[c] + 1)
                b0 = (c - groups[group_of[c]][0]) * BPC
                for t in range(TPC):
                    mm = pe.matmul(ps[:, t * P:(t + 1) * P], xaT[:, c % XA_RING, t * P:(t + 1) * P],
                                   mix[:, b0 + t * BPC // TPC, :], start=True, stop=True)
                mm.then_inc(attn_ps, 1)

            do = dict(transpose=transpose, route=route, rank=rank, gathered=gathered, out_turn=out_turn,
                      a_turn=a_turn, a_gram=a_gram, a_gq=a_gq, a_kq=a_kq, a_pv=a_pv, a_mix=a_mix, a_out=a_out)
            pe.wait_ge(const_in, 32)
            pe.wait_ge(bf_ready, 2)
            for n in range(-1, LAST + 1):
                if 0 <= n < NSLOT:
                    gate_up(n)
                for half in range(2):
                    if half == 1 and 2 <= n < NSLOT + 2:
                        down(n - 2)
                    for name, arg in stages.get(2 * n + half, ()):
                        if name in do:
                            do[name](arg)

        @block.scalar
        def _(act):
            act.dma_start(cst[:], consts).then_inc(const_in, 16)
            act.dma_start(wr[:], w_router).then_inc(const_in, 16)
            act.wait_ge(pool_const, 1)
            act.activation(warm[:], mhalf[:], ACT.Silu)
            act.wait_ge(const_in, 32)
            act.copy(wr_hi[:], wr[:]).then_inc(wr_hi_done, 1)

            def normalise(k, c, done):
                for t in range(TPC):
                    ins = act.activation(XN[:, c * TPC + t, 0:H], X[:, c * TPC + t, :], ACT.Identity,
                                         bias=shift[:, k, t:t + 1], scale=rstd[:, k, t:t + 1])
                ins.then_inc(done, 1)

            def apply(q):
                if q == 0:
                    return
                act.wait_ge(ln_pow, q + 1)
                if q >= CHUNKS:
                    act.wait_ge(gram_ps, group_of[q - CHUNKS] + 1)
                normalise(q, q % CHUNKS, xn_done)

            def a_apply(c):
                act.wait_ge(an_pow, c + 1)
                if c == 0:
                    act.wait_ge(dispatched[0], 16 * TOP * TILES)
                normalise(LAYERS * CHUNKS + c, c, xa_done)

            def silu(n):
                N = slots[n][4]
                act.wait_ge(gu_done, n + 1)
                if n >= 2:
                    act.wait_ge(hidden_done, n - 1)
                act.activation(S[:, n % 2, 0:N], psG[n % 2][:, 0:N], ACT.Silu).then_inc(silu_done, 1)

            def split(p):
                raw_ready(act, p)
                act.copy(wgu_hi[:, p * PIECE:(p + 1) * PIECE], raw[:, p % RAW_RING, :]).then_inc(hi_split, 1)

            def transpose(q):
                act.wait_ge(xT_turned, q + 1)
                act.copy(xT_hi[:, q % CHUNKS, :], psM[0][:]).then_inc(xT_hi_done, 1)

            def route(q):
                act.wait_ge(gap_done, q + 1)
                act.activation(tanh_gap[:, q % 2, :], gap[:, q % 2, :], ACT.Tanh, scale=0.5).then_inc(tanh_done, 1)

            def gathered(le):
                g = gidx(*le)
                act.wait_ge(xg_turned, g + 1)
                act.copy(xgT_hi[:, g % 2, :], psM[0][:, 0:CAP]).then_inc(xg_hi_done, 1)

            def out_copy(u):
                N = slots[last_slot[u]][4]
                act.wait_ge(down_done, last_slot[u] + 1)
                if u:
                    act.wait_ge(out_turned, u)
                act.copy(oT[:, 0:N], psD[u % 2][:, 0:N]).then_inc(out_copied, 1)

            def a_turn(c):
                act.wait_ge(xa_turned, c + 1)
                if c >= XA_RING:
                    act.wait_ge(attn_ps, c - XA_RING + 1)
                act.copy(xaT[:, c % XA_RING, :], psM[0][:]).then_inc(xaT_done, 1)

            def small(g, ps_done, bank, dst, done, used):
                act.wait_ge(ps_done, g + 1)
                if g >= 1:
                    act.wait_ge(used, g)
                nb = len(groups[g]) * BPC
                act.copy(dst[:, 0:nb].rearrange("p b q -> p (b q)"), psM[bank][:, 0:nb * P]).then_inc(done, 1)

            def a_gram(g):
                small(g, gram_ps, 1, gram, gram_sb, gq_ps)

            def a_gq(g):
                small(g, gq_ps, 0, gq, gq_sb, kq_ps)

            def a_soft(g):
                act.wait_ge(zs_done, g + 1)
                nb = len(groups[g]) * BPC
                act.activation(zt[:, 0:nb], zs[:, 0:nb], ACT.Tanh, scale=0.5 * SCALE).then_inc(zt_done, 1)

            def a_pv(g):
                small(g, pv_ps, 0, pv, pv_sb, mix_ps)

            def a_mix(g):
                act.wait_ge(mix_ps, g + 1)
                if g >= 1:
                    act.wait_ge(attn_ps, groups[g][0])
                small(g, mix_ps, 1, mix, mix_sb, mix_ps)

            do = dict(split=split, apply=apply, a_apply=a_apply, transpose=transpose, route=route, gathered=gathered, out_copy=out_copy,
                      a_turn=a_turn,
                      a_gram=a_gram, a_gq=a_gq, a_soft=a_soft, a_pv=a_pv, a_mix=a_mix)
            for n in range(-1, LAST + 1):
                for half in range(2):
                    if half == 1 and 0 <= n < NSLOT:
                        silu(n)
                    for name, arg in stages.get(2 * n + half, ()):
                        if name in do:
                            do[name](arg)

        @block.vector
        def _(dve):
            steps = [0]

            def then(ins):
                steps[0] += 1
                ins.then_inc(dve_step, 1)
                dve.wait_ge(dve_step, steps[0])

            def hidden(n):
                N = slots[n][4]
                dve.wait_ge(silu_done, n + 1)
                if n >= H_RING:
                    dve.wait_ge(down_done, n - H_RING + 1)
                dve.tensor_tensor(Hd[:, n % H_RING, 0:N], S[:, n % 2, 0:N], psU[n % 2][:, 0:N], ALU.mult)\
                    .then_inc(hidden_done, 1)

            def split(p):
                dve.wait_ge(hi_split, p + 1)
                cols = slice(p * PIECE, (p + 1) * PIECE)
                dve.tensor_tensor(wgu_lo[:, cols], raw[:, p % RAW_RING, :], wgu_hi[:, cols].bitcast(F32), ALU.subtract)\
                    .then_inc(lo_split, 1)

            def stats(k, c, done):
                for t in range(TPC):
                    ins = dve.bn_stats(stat[:, k, t, :], X[:, c * TPC + t, :])
                then(ins)
                for t in range(TPC):
                    ins = dve.bn_aggr(mv[:, k, t, :], stat[:, k, t, :])
                then(ins)
                dve.tensor_scalar(neg_mean[:, k, :], mv[:, k, :, 0], -1.0, None, ALU.mult)
                dve.tensor_scalar(var_eps[:, k, :], mv[:, k, :, 1], LN_EPS, None, ALU.add).then_inc(done, 1)

            def ln(q):
                if q < CHUNKS:
                    dve.wait_ge(x_in[q], 16)
                stats(q, q % CHUNKS, ln_stats)

            def apply(q):
                if q:
                    return
                dve.wait_ge(ln_pow, q + 1)
                for t in range(TPC):
                    ins = dve.tensor_scalar(XN[:, t, 0:H], X[:, t, :], mv[:, q, t, 0:1], rstd[:, q, t:t + 1],
                                            ALU.subtract, ALU.mult)
                ins.then_inc(xn_done, 1)

            def transpose(q):
                dve.wait_ge(xT_hi_done, q + 1)
                c = q % CHUNKS
                dve.tensor_tensor(xT_lo[:, c, :], psM[0][:], xT_hi[:, c, :].bitcast(F32), ALU.subtract)\
                    .then_inc(xT_lo_done, 1)

            def route(q):
                r = q % 2
                if q >= 2:
                    dve.wait_ge(ranks_done, q - 1)
                dve.wait_ge(rms_pow, q + 1)
                dve.wait_ge(logits_done, q + 1)
                ins = dve.tensor_tensor(logit[:], psM[1][:, 0:TPC * E].rearrange("p (t e) -> p t e", e=E),
                                        rrms[:, q, :].unsqueeze(2).to_broadcast([P, TPC, E]), ALU.mult)
                ins.then_inc(logits_read, 1)
                dve.wait_ge(logits_read, q + 1)
                for t in range(TPC):
                    ins = dve.max(top_v[:, r, t, :], logit[:, t, :])
                then(ins)
                dve.tensor_tensor(gap[:, r, :], top_v[:, r, :, 0], top_v[:, r, :, 1], ALU.subtract).then_inc(gap_done, 1)
                for t in range(TPC):
                    ins = dve.max_index(top_i[:, r, t, :], top_v[:, r, t, :], logit[:, t, :])
                then(ins)
                then(dve.tensor_tensor(choice[:, r], iota_e[:].unsqueeze(1).unsqueeze(1).to_broadcast([P, TOP, TPC, E]),
                                       top_i[:, r, :, 0:TOP].rearrange("p t k -> p k t").unsqueeze(3)
                                       .to_broadcast([P, TOP, TPC, E]), ALU.is_equal))
                ins = dve.tensor_tensor(mask[:, r], choice[:, r, 0], choice[:, r, 1], ALU.add)
                ins.then_inc(masks_done, 1)
                if q % CHUNKS < CHUNKS - 1:
                    dve.wait_ge(masks_done, q + 1)
                    then(dve.tensor_reduce(seen_c[:], mask[:, r].rearrange("p t e -> p e t"), AX.X, ALU.add))
                    if q % CHUNKS == 0:
                        then(dve.tensor_copy(seen[:, 1 - r], seen_c[:]))
                    else:
                        then(dve.tensor_tensor(seen[:, 1 - r], seen[:, r], seen_c[:], ALU.add))

            def rank(q):
                r, c = q % 2, q % CHUNKS
                dve.wait_ge(tanh_done, q + 1)
                rows = XN[:, tiles_of(c), :]
                dve.tensor_copy(rows[:, :, COL_E0], top_i[:, r, :, 0])
                dve.tensor_scalar(rows[:, :, COL_W1], tanh_gap[:, r, :], -0.25, 0.25, ALU.mult, ALU.add)
                then(dve.tensor_scalar(rows[:, :, COL_DW], tanh_gap[:, r, :], 0.5, None, ALU.mult))
                dve.wait_ge(ranks_done, q + 1)
                ps = psM[1][:, 0:TPC * E].rearrange("p (t e) -> p t e", e=E)
                dve.tensor_scalar(late[:], ps, float(CAP), float(FAR), ALU.is_ge, ALU.mult)
                ins = dve.tensor_tensor(place[:], ps, slot_base[:].unsqueeze(1).to_broadcast([P, TPC, E]), ALU.add)
                ins.then_inc(ranks_read, 1)
                dve.wait_ge(ranks_read, q + 1)
                then(dve.tensor_tensor(place[:], place[:], late[:], ALU.add))
                then(dve.tensor_tensor(picked[:], choice[:, r], place[:].unsqueeze(1).to_broadcast([P, TOP, TPC, E]),
                                       ALU.mult))
                then(dve.tensor_reduce(place_f[:], picked[:], AX.X, ALU.add))
                dve.tensor_scalar(place_u[:, q], place_f[:], float(E * CAP), None, ALU.min).then_inc(places_done, 1)

            def gathered(le):
                l, e = le
                g = gidx(l, e)
                r = g % XG_RING
                dve.wait_ge(xg_hi_done, g + 1)
                dve.tensor_tensor(xgT_lo[:, g % 2, :], psM[0][:, 0:CAP], xgT_hi[:, g % 2, :].bitcast(F32), ALU.subtract)\
                    .then_inc(xg_lo_done, 1)
                then(dve.tensor_scalar(wsl[:, r, :], xg[:, r, :, COL_E0], float(e), None, ALU.is_equal))
                then(dve.tensor_tensor(wsl[:, r, :], wsl[:, r, :], xg[:, r, :, COL_DW], ALU.mult))
                then(dve.tensor_tensor(wsl[:, r, :], wsl[:, r, :], xg[:, r, :, COL_W1], ALU.add))

            def out_turn(u):
                kind, l, i = units[u]
                dve.wait_ge(out_turned, u + 1)
                if kind == SHARED:
                    rows = X[:, tiles_of(i), :].rearrange("p t h -> p (t h)")
                    ins = dve.scalar_tensor_tensor(out=rows, in0=psM[1][:], scalar=0.5, in1=rows, op0=ALU.mult, op1=ALU.add)
                    ins.then_inc(out_read, 1)
                    dve.wait_ge(out_read, u + 1)
                else:
                    g = gidx(l, i)
                    if g >= 2:
                        dve.wait_ge(added, 16 * NB * (g - 1))
                    for j, (r0, n) in enumerate(BLOCKS):
                        ins = dve.tensor_scalar(yw[0:n, g % 2, j, :], psM[1][0:n, j * P:(j + 1) * P],
                                                wsl[0:n, g % XG_RING, j:j + 1], None, ALU.mult)
                    ins.then_inc(out_read, 1)

            def add_sums(k, c):
                dve.wait_ge(sums_in[k % 2], 16 * (k // 2 + 1))
                ins = dve.tensor_tensor(X[:, tiles_of(c), :], X[:, tiles_of(c), :], sums[:, k % 2], ALU.add)
                ins.then_inc(combined, 1)
                dve.wait_ge(combined, k + 1)

            def combine(c):
                add_sums(c, c)
                stats(LAYERS * CHUNKS + c, c, an_stats)

            def finish(c):
                add_sums(CHUNKS + c, c)

            def a_kq(g):
                nb = len(groups[g]) * BPC
                dve.wait_ge(kq_ps, g + 1)
                ins = dve.tensor_tensor(kq[:, 0:nb], psM[1][:, 0:nb * P].rearrange("p (b q) -> p b q", b=nb),
                                        block_mask.unsqueeze(1).to_broadcast([P, nb, P]), ALU.mult)
                ins.then_inc(kq_read, 1)
                dve.wait_ge(kq_read, g + 1)
                then(dve.tensor_reduce(zc[:, 0:nb], kq[:, 0:nb].rearrange("p b (g j) -> p b j g", j=HEAD), AX.X, ALU.add))
                then(dve.tensor_reduce(zmax[:, 0:nb], zc[:, 0:nb], AX.X, ALU.max))
                dve.tensor_tensor(zs[:, 0:nb], zc[:, 0:nb], zmax[:, 0:nb].unsqueeze(2).to_broadcast([P, nb, HEAD]),
                                  ALU.subtract).then_inc(zs_done, 1)

            def a_soft(g):
                nb = len(groups[g]) * BPC
                num, den, total = znum[:, 0:nb], zden[:, 0:nb], zsum[:, 0:nb]
                dve.wait_ge(zt_done, g + 1)
                dve.tensor_scalar(num, zt[:, 0:nb], 1.0, None, ALU.add)
                then(dve.tensor_scalar(den, zt[:, 0:nb], -1.0, 1.0, ALU.mult, ALU.add))
                then(dve.reciprocal(den, den))
                then(dve.tensor_tensor(num, num, den, ALU.mult))
                then(dve.tensor_reduce(total, num, AX.X, ALU.add))
                then(dve.reciprocal(total, total))
                then(dve.tensor_tensor(num, num, total.unsqueeze(2).to_broadcast([P, nb, HEAD]), ALU.mult))
                if g >= 1:
                    dve.wait_ge(pv_ps, g)
                for b in range(nb):
                    ins = dve.tensor_tensor(zb[:, b, :].rearrange("p (g j) -> p g j", j=HEAD),
                                            block_mask.rearrange("p (g j) -> p g j", j=HEAD),
                                            znum[:, b, :].unsqueeze(1).to_broadcast([P, P // HEAD, HEAD]), ALU.mult)
                ins.then_inc(zb_done, 1)

            def a_out(c):
                dve.wait_ge(attn_ps, c + 1)
                rows = X[:, tiles_of(c), :].rearrange("p t h -> p (t h)")
                ins = dve.tensor_tensor(rows, psM[0][:], rows, ALU.add)
                ins.then_inc(attn_added, 1)
                dve.wait_ge(attn_added, c + 1)

            do = dict(split=split, ln=ln, apply=apply, transpose=transpose, route=route, rank=rank, gathered=gathered,
                      out_turn=out_turn, combine=combine, finish=finish, a_kq=a_kq, a_soft=a_soft,
                      a_out=a_out)
            def start():
                dve.wait_ge(const_in, 32)
                dve.tensor_copy(tri[:], cst[:, 2 * P:3 * P]).then_inc(bf_ready, 1)
                dve.memset(ones[:], 1.0).then_inc(bf_ready, 1)
                dve.wait_ge(wr_hi_done, 1)
                dve.tensor_tensor(wr_lo[:], wr[:], wr_hi[:].bitcast(F32), ALU.subtract).then_inc(wr_done, 1)
                dve.memset(zeros[:], 0.0).then_inc(dve_const, 1)
                dve.wait_ge(pool_const, 3)

            for n in range(-1, LAST + 1):
                for half in range(2):
                    if half == 1 and 0 <= n < NSLOT:
                        hidden(n)
                    for name, arg in stages.get(2 * n + half, ()):
                        if name in do:
                            do[name](arg)
                        if (name, arg) == ("ln", 1):
                            start()

        @block.gpsimd
        def _(pool):
            steps = [0]

            def then(ins):
                steps[0] += 1
                ins.then_inc(pool_step, 1)
                pool.wait_ge(pool_step, steps[0])

            pool.memset(mhalf[:], -0.5).then_inc(pool_const, 1)
            then(pool.memset(init_row[:], 0.0))
            pool.iota(init_row[:, COL_ID:COL_ID + 1].bitcast(U32), pattern=[[0, 1]], base=T, channel_multiplier=1)\
                .then_inc(pool_const, 1)
            then(pool.iota(XN[:, :, COL_ID].bitcast(U32), pattern=[[P, TILES]], base=0, channel_multiplier=1))
            then(pool.iota(iota_e[:], pattern=[[1, E]], base=0, channel_multiplier=0, allow_small_or_imprecise_dtypes=True))
            then(pool.iota(slot_base[:], pattern=[[CAP, E]], base=0, channel_multiplier=0, allow_small_or_imprecise_dtypes=True))
            then(pool.memset(wsl[:], 0.0))
            pool.memset(xg[:], 0.0).then_inc(pool_const, 1)
            pool.wait_ge(pool_const, 3)

            def rsqrt_var(k, done):
                ins = pool.tensor_tensor(rstd[:, k], var_eps[:, k], mhalf[:], ALU.pow)
                then(ins)
                pool.tensor_tensor(shift[:, k], neg_mean[:, k], rstd[:, k], ALU.mult).then_inc(done, 1)

            def ffn_pow(q):
                pool.wait_ge(ln_stats, q + 1)
                rsqrt_var(q, ln_pow)

            def ffn_rms(q):
                then(pool.tensor_tensor(msq[:, q], rstd[:, q], rstd[:, q], ALU.mult))
                then(pool.tensor_tensor(msq[:, q], msq[:, q], mv[:, q, :, 1], ALU.mult))
                then(pool.tensor_scalar(msq[:, q], msq[:, q], RMS_EPS, None, ALU.add))
                pool.tensor_tensor(rrms[:, q], msq[:, q], mhalf[:], ALU.pow).then_inc(rms_pow, 1)

            def attn_pow(c):
                pool.wait_ge(an_stats, c + 1)
                rsqrt_var(LAYERS * CHUNKS + c, an_pow)

            def dispatch(q, tiles=range(TPC)):
                l, c = q // CHUNKS, q % CHUNKS
                pool.wait_ge(places_done, q + 1)
                if c == 0:
                    pool.wait_ge(rows_init[l], 16)
                for t in tiles:
                    for k in range(TOP):
                        pool.indirect_dma_start(
                            out=rows_dram[l], out_offset=bass.IndirectOffsetOnAxis(ap=place_u[:, q, k, t:t + 1], axis=0),
                            in_=XN[:, c * TPC + t, :], in_offset=None, bounds_check=E * CAP - 1, oob_is_err=False,
                        ).then_inc(dispatched[l], 16)

            def add_outputs(l, e):
                g = gidx(l, e)
                pool.wait_ge(out_read, unit_of[(EXPERT, l, e)] + 1)
                if e == 0:
                    pool.wait_ge(sums_init[l], 16 * (CHUNKS + 1))
                if g:
                    pool.wait_ge(added, 16 * NB * g)
                for j, (r0, n) in enumerate(BLOCKS):
                    pool.indirect_dma_start(
                        out=sums_dram[l],
                        out_offset=bass.IndirectOffsetOnAxis(ap=xg[0:n, g % XG_RING, j, COL_ID:COL_ID + 1].bitcast(U32), axis=0),
                        in_=yw[0:n, g % 2, j, :], in_offset=None, compute_op=ALU.add,
                    ).then_inc(added, 16)

            ffn_pow(0)
            ffn_pow(1)
            ffn_rms(0)
            ffn_pow(2)
            ffn_rms(1)
            ffn_pow(3)
            dispatch(0)
            ffn_rms(2)
            dispatch(1)
            ffn_rms(3)
            dispatch(2)
            dispatch(3)
            for e in range(E):
                add_outputs(0, e)
            attn_pow(0)
            attn_pow(1)
            ffn_pow(4)
            ffn_pow(5)
            ffn_rms(4)
            attn_pow(2)
            ffn_rms(5)
            dispatch(4, range(0, 1))
            attn_pow(3)
            dispatch(4, range(1, 3))
            ffn_pow(6)
            ffn_rms(6)
            dispatch(4, range(3, 4))
            dispatch(5, range(0, 3))
            ffn_pow(7)
            ffn_rms(7)
            dispatch(5, range(3, 4))
            dispatch(6)
            dispatch(7)
            for e in range(E):
                add_outputs(1, e)


def kernel(**inputs):
    import numpy as np
    import concourse.bacc as bacc
    from concourse import mybir as _mybir
    from concourse.bass_utils import run_bass_kernel_spmd

    a = {k: np.asarray(v) for k, v in inputs.items()}
    x = a["L0_attn_x"]
    B, S, H = x.shape
    T = B * S
    E = a["L0_ffn_rg"].shape[0]

    def hidden_last(w):
        w = w.reshape(-1, H, w.shape[-1] // P, P)
        return w.transpose(1, 0, 2, 3).reshape(H, -1, P)

    def hidden_first(w):
        return w.reshape(-1, P, H).transpose(1, 0, 2)

    gate = np.concatenate([hidden_last(a["L0_ffn_sg"]), hidden_last(a["L0_ffn_rg"])], axis=1)
    up = np.concatenate([hidden_last(a["L0_ffn_su"]), hidden_last(a["L0_ffn_ru"])], axis=1)
    down = np.concatenate([hidden_first(a["L0_ffn_sd"]), hidden_first(a["L0_ffn_rd"])], axis=1)
    r = np.arange(P)
    consts = np.concatenate([r[:, None] == r, r[:, None] // 8 == r // 8, r[:, None] < r], axis=1)
    arrays = {
        "x": x.reshape(T, H),
        "w_gate_up": np.stack([gate, up], axis=2).reshape(H, -1),
        "w_down": down.reshape(P, -1),
        "w_attn": np.concatenate([a["L0_attn_Wq"].T, a["L0_attn_Wk"].T, a["L0_attn_Wv"], a["L0_attn_Wo"].T], axis=1),
        "w_router": a["L0_ffn_router_w"].T,
        "consts": consts.astype(np.float32),
    }
    arrays = {k: np.ascontiguousarray(v) for k, v in arrays.items()}
    nc = bacc.Bacc("TRN2", target_bir_lowering=False, num_devices=1)
    args = [nc.dram_tensor(k, v.shape, _mybir.dt.from_np(v.dtype), kind="ExternalInput").ap() for k, v in arrays.items()]
    out = nc.dram_tensor("out", (T, H), _mybir.dt.float32, kind="ExternalOutput").ap()
    macaron_block_kernel(nc, *args, out)
    res = run_bass_kernel_spmd(nc, [arrays], core_ids=[0])
    return res.results[0]["out"].reshape(B, S, H)
```

```python
from contextlib import ExitStack

import concourse.bass as bass
from concourse import mybir

ALU = mybir.AluOpType
ACT = mybir.ActivationFunctionType
AX = mybir.AxisListType
F32 = mybir.dt.float32
F32R = mybir.dt.float32r
BF16 = mybir.dt.bfloat16
U32 = mybir.dt.uint32

P = 128


TENSOR_STAGES = (
    (-4, "transpose", 0), (-1, "route", 0), (0, "rank", 0), (3, "transpose", 1), (5, "route", 1), (7, "transpose", 2),
    (9, "rank", 1), (10, "route", 2), (12, "transpose", 3), (13, "rank", 2), (15, "route", 3), (18, "rank", 3),
    (121, "a_turn", 0), (121, "a_gram", 0), (122, "a_gq", 0), (123, "a_kq", 0), (124, "a_gram", 1),
    (124, "a_turn", 1), (125, "a_gq", 1), (126, "a_kq", 1), (126, "a_pv", 0), (127, "a_turn", 2), (127, "a_mix", 0),
    (127, "a_out", 0), (127, "a_gram", 2), (127, "a_pv", 1), (127, "a_mix", 1), (127, "a_gq", 2), (127, "a_out", 1),
    (127, "a_kq", 2), (127, "transpose", 4), (127, "route", 4), (127, "a_pv", 2), (128, "rank", 4), (129, "a_mix", 2),
    (131, "transpose", 5), (135, "route", 5), (135, "a_out", 2), (137, "a_gram", 3), (137, "a_turn", 3),
    (137, "rank", 5), (138, "a_gq", 3), (139, "a_kq", 3), (140, "transpose", 6), (142, "route", 6), (143, "a_pv", 3),
    (144, "rank", 6), (145, "a_mix", 3), (146, "a_out", 3), (153, "transpose", 7), (154, "route", 7),
    (157, "rank", 7),
)
SCALAR_STAGES = (
    (-9, "split", 0), (-3, "transpose", 0), (-3, "split", 1), (-2, "apply", 1), (1, "gate", 0), (2, "split", 2),
    (3, "transpose", 1), (6, "split", 3), (6, "apply", 2), (7, "transpose", 2), (9, "gate", 1), (11, "apply", 3),
    (12, "transpose", 3), (13, "gate", 2), (18, "gate", 3), (20, "split", 4), (22, "split", 5), (24, "split", 6),
    (26, "split", 7), (28, "split", 8), (30, "split", 9), (38, "split", 10), (40, "split", 11), (42, "split", 12),
    (44, "split", 13), (46, "split", 14), (48, "split", 15), (50, "split", 16), (52, "split", 17), (54, "split", 18),
    (56, "split", 19), (120, "a_apply", 0), (122, "a_gram", 0), (122, "a_turn", 0), (124, "a_gq", 0),
    (124, "a_apply", 1), (124, "a_exp", 0), (126, "a_gram", 1), (126, "a_turn", 1), (126, "a_apply", 2),
    (126, "a_gq", 1), (128, "a_pv", 0), (128, "a_exp", 1), (128, "a_turn", 2), (128, "a_mix", 0), (128, "a_gram", 2),
    (128, "a_pv", 1), (128, "a_mix", 1), (128, "a_gq", 2), (128, "apply", 4), (128, "transpose", 4),
    (128, "a_exp", 2), (128, "a_pv", 2), (128, "gate", 4), (130, "apply", 5), (132, "transpose", 5),
    (132, "a_mix", 2), (136, "a_apply", 3), (138, "gate", 5), (138, "a_gram", 3), (138, "a_turn", 3),
    (140, "a_gq", 3), (140, "apply", 6), (140, "a_exp", 3), (140, "transpose", 6), (144, "a_pv", 3), (144, "gate", 6),
    (146, "a_mix", 3), (152, "apply", 7), (154, "transpose", 7), (156, "gate", 7),
)
VECTOR_STAGES = (
    (-10, "ln", 0), (-10, "ln_var", 0), (-9, "split", 0), (-8, "ln", 1), (-7, "apply", 0), (-6, "ln_var", 1),
    (-5, "ln", 2), (-5, "start", 0), (-4, "ln_var", 2), (-4, "transpose", 0), (-4, "rms", 0), (-3, "split", 1),
    (-2, "ln", 3), (-2, "ln_var", 3), (0, "best", 0), (0, "choose", 0), (0, "rms", 1), (1, "rank", 0),
    (1, "place", 0), (2, "split", 2), (3, "transpose", 1), (3, "rms", 2), (5, "rms", 3), (6, "split", 3),
    (6, "best", 1), (7, "choose", 1), (8, "transpose", 2), (10, "rank", 1), (10, "place", 1), (11, "best", 2),
    (11, "choose", 2), (13, "transpose", 3), (14, "rank", 2), (14, "place", 2), (16, "best", 3), (16, "choose", 3),
    (19, "rank", 3), (19, "place", 3), (20, "split", 4), (22, "split", 5), (24, "split", 6), (26, "split", 7),
    (28, "split", 8), (30, "split", 9), (38, "split", 10), (40, "split", 11), (42, "split", 12), (44, "split", 13),
    (46, "split", 14), (48, "split", 15), (50, "split", 16), (52, "split", 17), (54, "split", 18), (56, "split", 19),
    (116, "combine", 0), (116, "a_stats", 0), (117, "a_var", 0), (120, "combine", 1), (120, "combine", 2),
    (120, "a_stats", 1), (120, "a_stats", 2), (122, "a_var", 1), (122, "combine", 3), (124, "a_var", 2),
    (124, "a_kq", 0), (124, "a_own", 0), (124, "a_exp", 0), (126, "a_norm", 0), (126, "a_kq", 1), (126, "a_own", 1),
    (128, "a_exp", 1), (128, "a_norm", 1), (128, "a_out", 0), (128, "ln", 4), (128, "ln_var", 4), (128, "rms", 4),
    (128, "a_out", 1), (128, "a_kq", 2), (128, "a_own", 2), (128, "ln", 5), (128, "transpose", 4), (128, "a_exp", 2),
    (128, "a_norm", 2), (128, "best", 4), (128, "choose", 4), (128, "ln_var", 5), (128, "rank", 4), (128, "place", 4),
    (128, "rms", 5), (132, "a_stats", 3), (134, "a_var", 3), (134, "transpose", 5), (136, "best", 5),
    (136, "a_out", 2), (136, "choose", 5), (138, "ln", 6), (138, "ln_var", 6), (138, "rms", 6), (138, "rank", 5),
    (140, "place", 5), (140, "a_kq", 3), (140, "a_own", 3), (140, "a_exp", 3), (140, "transpose", 6),
    (142, "a_norm", 3), (144, "best", 6), (144, "choose", 6), (144, "rank", 6), (144, "place", 6), (148, "a_out", 3),
    (148, "ln", 7), (148, "ln_var", 7), (148, "rms", 7), (154, "transpose", 7), (154, "best", 7), (156, "choose", 7),
    (158, "rank", 7), (158, "place", 7), (251, "finish", 0), (253, "finish", 1), (255, "finish", 2),
    (258, "finish", 3),
)
POOL_STAGES = (
    ("ffn_pow", 0), ("ffn_pow", 1), ("ffn_rms", 0), ("ffn_pow", 2), ("ffn_pow", 3), ("ffn_rms", 1), ("dispatch", 0),
    ("ffn_rms", 2), ("dispatch", 1), ("ffn_rms", 3), ("dispatch", 2), ("dispatch", 3), ("add_outputs", 0, 0),
    ("add_outputs", 0, 1), ("add_outputs", 0, 2), ("add_outputs", 0, 3), ("add_outputs", 0, 4), ("add_outputs", 0, 5),
    ("add_outputs", 0, 6), ("add_outputs", 0, 7), ("attn_pow", 0), ("attn_pow", 1), ("attn_pow", 2), ("ffn_pow", 4),
    ("ffn_rms", 4), ("ffn_pow", 5), ("dispatch", 4, (0,)), ("ffn_rms", 5), ("dispatch", 4, (1, 2)), ("attn_pow", 3),
    ("dispatch", 4, (3,)), ("ffn_pow", 6), ("ffn_rms", 6), ("dispatch", 5), ("dispatch", 6, (0, 1, 2)),
    ("ffn_pow", 7), ("ffn_rms", 7), ("dispatch", 6, (3,)), ("dispatch", 7), ("add_outputs", 1, 0),
    ("add_outputs", 1, 1), ("add_outputs", 1, 2), ("add_outputs", 1, 3), ("add_outputs", 1, 4), ("add_outputs", 1, 5),
    ("add_outputs", 1, 6), ("add_outputs", 1, 7),
)


def macaron_block_kernel(nc, x, w_gate_up, w_down, w_attn, w_router, consts, out):
    T, H = x.shape
    LAYERS = 2
    E = w_router.shape[1]
    HT = w_down.shape[1] // P
    HT_EXPERT = 4 * H // P
    HT_SHARED = HT - E * HT_EXPERT
    CAP = max(int(1.25 * T / E), 1)
    TILES = T // P
    TPC = 4
    CHUNKS = TILES // TPC
    C = TPC * P
    SEQ = 2 * P
    BPC = C // SEQ
    HEAD = 8
    TOP = 2
    EARLY_TILES = 4
    QS = LAYERS * CHUNKS
    BLOCKS = [(j * P, min(P, CAP - j * P)) for j in range((CAP + P - 1) // P)]
    NB = len(BLOCKS)
    ROW = H + 4
    COL_ID, COL_E0, COL_W1, COL_DW = H, H + 1, H + 2, H + 3
    FAR = 4096
    LN_EPS = 1e-5
    RMS_EPS = 1.1920928955078125e-07
    SCALE = float(HEAD) ** -0.5
    HPP = 2
    PIECES = HT // HPP
    PIECE = HPP * 2 * P
    RAW_RING, XG_RING, H_RING, XA_RING = 4, 6, 3, 3

    SHARED, EXPERT = "shared", "expert"
    experts = [(EXPERT, e) for e in range(E)]
    shared = [(SHARED, (c, 0, HT_SHARED)) for c in range(CHUNKS)]
    cut = [(SHARED, (2, 0, EARLY_TILES)), (SHARED, (2, EARLY_TILES, HT_SHARED - EARLY_TILES))]
    order = [shared[:2] + cut[:1] + experts + cut[1:] + shared[3:], shared[:3] + experts + shared[3:]]
    units, slots, first_slot, last_slot = [], [], {}, {}
    for l in range(LAYERS):
        for kind, i in order[l]:
            u = len(units)
            units.append((kind, l, i))
            base, tiles = i[1:] if kind == SHARED else (HT_SHARED + i * HT_EXPERT, HT_EXPERT)
            first_slot[u] = len(slots)
            for k in range(tiles):
                slots.append((u, k, tiles, base + k, C if kind == SHARED else CAP))
            last_slot[u] = len(slots) - 1
    unit_of = {v: u for u, v in enumerate(units)}
    NSLOT = len(slots)

    PE, ACTE, DVE = range(3)
    stages = ({}, {}, {})

    def at(engine, half_slot, name, arg):
        stages[engine].setdefault(half_slot, []).append((name, arg))

    for engine in (PE, ACTE, DVE):
        for u, (kind, l, i) in enumerate(units):
            if kind == SHARED:
                at(engine, 2 * (last_slot[u] + 2) + 1, "out_add", u)
            else:
                at(engine, 2 * (last_slot[u] + 2) + 1, "out_copy", u)
                at(engine, 2 * (last_slot[u] + 3), "out_turn", u)
                at(engine, 2 * first_slot[u] - (2 if (l, i) == (0, 0) else 3), "gathered", (l, i))
    for engine, table in ((PE, TENSOR_STAGES), (ACTE, SCALAR_STAGES), (DVE, VECTOR_STAGES)):
        for half_slot, name, arg in table:
            at(engine, half_slot, name, arg)
    FIRST, LAST = min(min(s) for s in stages) // 2, max(max(s) for s in stages) // 2

    with ExitStack() as ctx:
        def sb(name, shape, dt=F32):
            return ctx.enter_context(nc.sbuf_tensor(name, shape, dt))

        def pb(name, shape):
            return ctx.enter_context(nc.psum_tensor(name, shape, F32))

        def sem(name):
            return ctx.enter_context(nc.semaphore(name))

        rows_dram = [nc.dram_tensor(f"rows_{l}", [E * CAP, ROW], F32, kind="Internal").ap() for l in range(LAYERS)]
        sums_dram = [nc.dram_tensor(f"sums_{l}", [T + P, H], F32, kind="Internal").ap() for l in range(LAYERS)]

        cst = sb("cst", [P, 3 * P])
        ident, block_mask = cst[:, 0:P], cst[:, P:2 * P]
        wa = sb("wa", [P, 4 * P])
        wqT, wkT, wv, woT = (wa[:, i * P:(i + 1) * P] for i in range(4))
        wr = sb("wr", [P, E])
        wr_parts = sb("wr_parts", [P, 2, 2, E], F32R)
        tri = sb("tri", [P, P], BF16)
        ones = sb("ones", [P, P], BF16)
        iota_e = sb("iota_e", [P, E])
        slot_base = sb("slot_base", [P, E])
        mhalf = sb("mhalf", [P, TPC])
        quarter = sb("quarter", [P, 1])
        warm = sb("warm", [P, TPC])
        init_row = sb("init_row", [P, ROW])
        zeros = sb("zeros", [P, C])

        raw = sb("raw", [P, RAW_RING, PIECE])
        wgu_hi = sb("wgu_hi", [P, HT * 2 * P], F32R)
        wgu_lo = sb("wgu_lo", [P, HT * 2 * P], F32R)
        wd = sb("wd", [P, HT * P])

        X = sb("X", [P, TILES, H])
        XN = sb("XN", [P, TILES, ROW])
        xT_hi = sb("xT_hi", [P, T], F32R)
        xT_lo = sb("xT_lo", [P, T], F32R)
        S = sb("S", [P, 2, C])
        Hd = sb("Hd", [P, H_RING, C])
        oT = sb("oT", [P, CAP])
        xg = sb("xg", [P, XG_RING, NB, ROW])
        xgT_hi = sb("xgT_hi", [P, 2, CAP], F32R)
        xgT_lo = sb("xgT_lo", [P, 2, CAP], F32R)
        wsl = sb("wsl", [P, XG_RING, NB])
        yw = sb("yw", [P, 2, NB, H])
        sums = sb("sums", [P, 2, TPC, H])

        stat = sb("stat", [P, LAYERS + 1, TILES, 6])
        mv = sb("mv", [P, LAYERS + 1, TILES, 2])
        var_eps = sb("var_eps", [P, LAYERS + 1, TILES])
        rstd = sb("rstd", [P, LAYERS + 1, TILES])
        neg_mean = sb("neg_mean", [P, LAYERS + 1, TILES])
        shift = sb("shift", [P, LAYERS + 1, TILES])
        msq = sb("msq", [P, LAYERS, TILES])
        inv_var = sb("inv_var", [P, LAYERS, TILES])
        half_rrms = sb("half_rrms", [P, LAYERS, TILES])
        logit = sb("logit", [P, TPC, E])
        top_v = sb("top_v", [P, TPC, 8])
        top_i = sb("top_i", [P, TPC, 8], U32)
        choice = sb("choice", [P, 2, TOP, TPC, E])
        mask = sb("mask", [P, LAYERS, TILES, E], BF16)
        seen = sb("seen", [P, QS, E], BF16)
        gap = sb("gap", [P, QS, TPC])
        tanh_gap = sb("tanh_gap", [P, QS, TPC])
        late = sb("late", [P, TPC, E])
        place = sb("place", [P, TPC, E])
        picked = sb("picked", [P, TOP, TPC, E])
        place_f = sb("place_f", [P, TOP, TPC])
        place_u = sb("place_u", [P, LAYERS, TOP, TILES], U32)

        xaT = sb("xaT", [P, XA_RING, C])
        gram = sb("gram", [P, BPC, P])
        gq = sb("gq", [P, BPC, P])
        kq = sb("kq", [P, BPC, P])
        zc = sb("zc", [P, BPC, HEAD])
        zmax = sb("zmax", [P, BPC])
        zs = sb("zs", [P, BPC, HEAD])
        zt = sb("zt", [P, BPC, HEAD])
        znum = sb("znum", [P, BPC, HEAD])
        zden = sb("zden", [P, BPC, HEAD])
        zsum = sb("zsum", [P, BPC])
        zb = sb("zb", [P, BPC, P])
        pv = sb("pv", [P, BPC, P])
        mix = sb("mix", [P, BPC, P])

        psG = [pb(f"psG{i}", [P, C]) for i in range(2)]
        psU = [pb(f"psU{i}", [P, C]) for i in range(2)]
        psD = [pb(f"psD{i}", [P, C]) for i in range(2)]
        psM = [pb(f"psM{i}", [P, C]) for i in range(2)]

        const_in = sem("const_in")
        x_in = [sem(f"x_in{c}") for c in range(CHUNKS)]
        attn_in = sem("attn_in")
        down_in = [sem(f"down_in{i}") for i in range(2)]
        raw_in = [sem(f"raw_in{i}") for i in range(RAW_RING)]
        hi_split, lo_split = sem("hi_split"), sem("lo_split")
        bf_ready = sem("bf_ready")
        pool_const, dve_const = sem("pool_const"), sem("dve_const")
        rows_init = [sem(f"rows_init{l}") for l in range(LAYERS)]
        sums_init = [sem(f"sums_init{l}") for l in range(LAYERS)]
        msq_done, rms_pow = sem("msq_done"), sem("rms_pow")
        wr_hi_done, wr_done = sem("wr_hi_done"), sem("wr_done")
        gu_done, silu_done, hidden_done, down_done = sem("gu_done"), sem("silu_done"), sem("hidden_done"), sem("down_done")
        out_copied, out_turned = sem("out_copied"), sem("out_turned")
        out_read, logits_read, ranks_read = sem("out_read"), sem("logits_read"), sem("ranks_read")
        kq_read, attn_added = sem("kq_read"), sem("attn_added")
        dve_step, pool_step = sem("dve_step"), sem("pool_step")
        gates_done = sem("gates_done")
        ln_stats, ln_pow, xn_done = sem("ln_stats"), sem("ln_pow"), sem("xn_done")
        an_stats, an_pow, xa_done = sem("an_stats"), sem("an_pow"), sem("xa_done")
        xT_turned, xT_hi_done, xT_lo_done = sem("xT_turned"), sem("xT_hi_done"), sem("xT_lo_done")
        logits_done, masks_done, gap_done, tanh_done = sem("logits_done"), sem("masks_done"), sem("gap_done"), sem("tanh_done")
        ranks_done, places_done = sem("ranks_done"), sem("places_done")
        dispatched = [sem(f"dispatched{l}") for l in range(LAYERS)]
        rows_in = [sem(f"rows_in{i}") for i in range(XG_RING)]
        xg_turned, xg_hi_done, xg_lo_done = sem("xg_turned"), sem("xg_hi_done"), sem("xg_lo_done")
        added = sem("added")
        sums_in = [sem(f"sums_in{i}") for i in range(2)]
        combined = sem("combined")
        xa_turned, xaT_done = sem("xa_turned"), sem("xaT_done")
        gram_ps, gram_sb, gq_ps, gq_sb, kq_ps = sem("gram_ps"), sem("gram_sb"), sem("gq_ps"), sem("gq_sb"), sem("kq_ps")
        zs_done, zt_done, zb_done = sem("zs_done"), sem("zt_done"), sem("zb_done")
        pv_ps, pv_sb, mix_ps, mix_sb, attn_ps = sem("pv_ps"), sem("pv_sb"), sem("mix_ps"), sem("mix_sb"), sem("attn_ps")
        stored = sem("stored")

        x_t = x.rearrange("(t p) h -> p t h", p=P)
        out_t = out.rearrange("(t p) h -> p t h", p=P)

        def tiles_of(c):
            return slice(c * TPC, (c + 1) * TPC)

        def experts_before(u):
            return sum(kind == EXPERT for kind, _, _ in units[:u])

        def gidx(l, e):
            return l * E + e

        def raw_ready(eng, p):
            eng.wait_ge(raw_in[p % RAW_RING], 16 * (p // RAW_RING + 1))

        block = ctx.enter_context(nc.Block())

        @block.sync
        def _(sp):
            def piece(p):
                if p >= RAW_RING:
                    sp.wait_ge(lo_split, p - RAW_RING + 1)
                sp.dma_start(raw[:, p % RAW_RING, :], w_gate_up[:, p * PIECE:(p + 1) * PIECE])\
                    .then_inc(raw_in[p % RAW_RING], 16)

            def load_x(c):
                sp.dma_start(X[:, tiles_of(c), :], x_t[:, tiles_of(c), :]).then_inc(x_in[c], 16)

            def init_rows(l):
                sp.dma_start(rows_dram[l].rearrange("(i p) c -> p i c", p=P),
                             init_row[:].unsqueeze(1).to_broadcast([P, E * CAP // P, ROW])).then_inc(rows_init[l], 16)

            def init_sums(l):
                for c in range(CHUNKS):
                    sp.dma_start(sums_dram[l][c * C:(c + 1) * C, :].rearrange("(p t) h -> p (t h)", p=P), zeros[:])\
                        .then_inc(sums_init[l], 16)
                sp.dma_start(sums_dram[l][T:T + P, :], zeros[:, 0:H]).then_inc(sums_init[l], 16)

            load_x(0)
            piece(0)
            load_x(1)
            load_x(2)
            load_x(3)
            piece(1)
            sp.dma_start(wd[:, 0:HT_SHARED * P], w_down[:, 0:HT_SHARED * P]).then_inc(down_in[0], 16)
            piece(2)
            piece(3)
            sp.wait_ge(pool_const, 2)
            init_rows(0)
            for p in range(4, 8):
                piece(p)
            sp.dma_start(wd[:, HT_SHARED * P:], w_down[:, HT_SHARED * P:]).then_inc(down_in[1], 16)
            sp.wait_ge(dve_const, 1)
            init_sums(0)
            for p in range(8, 12):
                piece(p)
            sp.dma_start(wa[:], w_attn).then_inc(attn_in, 16)
            for p in range(12, PIECES - 6):
                piece(p)
            for l in range(LAYERS):
                for e in range(E):
                    g = gidx(l, e)
                    if l == 0 and 2 <= e <= 4:
                        for p in range(PIECES - 10 + 2 * e, PIECES - 8 + 2 * e):
                            piece(p)
                    if e == 0:
                        sp.wait_ge(dispatched[l], 16 * TOP * TILES)
                    if g >= XG_RING:
                        sp.wait_ge(added, 16 * NB * (g - XG_RING + 1))
                    full = CAP // P
                    sp.dma_start(xg[:, g % XG_RING, 0:full, :],
                                 rows_dram[l][e * CAP:e * CAP + full * P, :].rearrange("(j p) c -> p j c", p=P))\
                        .then_inc(rows_in[g % XG_RING], 16)
                    for r0, n in BLOCKS[full:]:
                        sp.dma_start(xg[0:n, g % XG_RING, full, :],
                                     rows_dram[l][e * CAP + r0:e * CAP + r0 + n, :]).then_inc(rows_in[g % XG_RING], 16)
                if l == 0:
                    init_rows(1)
                    init_sums(1)
                sp.wait_ge(added, 16 * NB * E * (l + 1))
                for c in range(CHUNKS):
                    k = l * CHUNKS + c
                    if k >= 2:
                        sp.wait_ge(combined, k - 1)
                    sp.dma_start(sums[:, k % 2, :, :],
                                 sums_dram[l][c * C:(c + 1) * C, :].rearrange("(t p) h -> p t h", p=P))\
                        .then_inc(sums_in[k % 2], 16)
            for c in range(CHUNKS):
                sp.wait_ge(combined, CHUNKS + c + 1)
                sp.wait_ge(out_read, 1 + max(u for u, (kind, l, i) in enumerate(units)
                                             if kind == SHARED and l == LAYERS - 1 and i[0] == c))
                sp.dma_start(out_t[:, tiles_of(c), :], X[:, tiles_of(c), :]).then_inc(stored, 16)
            sp.wait_ge(stored, 16 * CHUNKS)

        @block.tensor
        def _(pe):
            reader = [None, None]

            def take(bank, *read):
                if reader[bank]:
                    pe.wait_ge(*reader[bank])
                reader[bank] = read
                return psM[bank]

            def gate_up(n):
                u, k, tiles, ht, N = slots[n]
                kind, l, i = units[u]
                if n >= 2:
                    pe.wait_ge(hidden_done, n - 1)
                if l == 0 and (kind == EXPERT or i[0] == 0):
                    pe.wait_ge(lo_split, ht // HPP + 1)
                if k == 0:
                    if kind == SHARED:
                        pe.wait_ge(xT_lo_done, l * CHUNKS + i[0] + 1)
                    else:
                        pe.wait_ge(xg_lo_done, gidx(l, i) + 1)
                if kind == SHARED:
                    tokens = slice(i[0] * C, (i[0] + 1) * C)
                    hi, lo = xT_hi[:, tokens], xT_lo[:, tokens]
                else:
                    hi, lo = xgT_hi[:, gidx(l, i) % 2, :], xgT_lo[:, gidx(l, i) % 2, :]
                for half, ps in ((0, psG[n % 2]), (1, psU[n % 2])):
                    o = (2 * ht + half) * P
                    pe.matmul(ps[:, 0:N], wgu_hi[:, o:o + P], hi, start=True, stop=False)
                    pe.matmul(ps[:, 0:N], wgu_hi[:, o:o + P], lo, start=False, stop=False)
                    mm = pe.matmul(ps[:, 0:N], wgu_lo[:, o:o + P], hi, start=False, stop=True)
                mm.then_inc(gu_done, 1)

            def down(n):
                u, k, tiles, ht, N = slots[n]
                pe.wait_ge(hidden_done, n + 1)
                if k == 0 and u >= 2:
                    if units[u - 2][0] == SHARED:
                        pe.wait_ge(out_read, u - 1)
                    else:
                        pe.wait_ge(out_copied, experts_before(u - 1))
                if u == 0 and k == 0:
                    pe.wait_ge(down_in[0], 16)
                if units[u][0] == EXPERT and k == 0:
                    pe.wait_ge(down_in[1], 16)
                if units[u][0] == SHARED:
                    for t in range(TPC):
                        tokens = slice(t * P, (t + 1) * P)
                        mm = pe.matmul(psD[u % 2][:, tokens], Hd[:, n % H_RING, tokens], wd[:, ht * P:(ht + 1) * P],
                                       start=(k == 0 and t == 0), stop=(k == tiles - 1), skip_group_check=True)
                else:
                    mm = pe.matmul(psD[u % 2][:, 0:N], wd[:, ht * P:(ht + 1) * P], Hd[:, n % H_RING, 0:N],
                                   start=(k == 0), stop=(k == tiles - 1))
                mm.then_inc(down_done, 1)

            def transpose(q):
                c = q % CHUNKS
                ps = take(0, xT_lo_done, q + 1)
                pe.wait_ge(xn_done, q + 1)
                for t in range(TPC):
                    mm = pe.transpose(ps[:, t * P:(t + 1) * P], XN[:, c * TPC + t, 0:H], ident)
                mm.then_inc(xT_turned, 1)

            def route(q):
                pe.wait_ge(xT_lo_done, q + 1)
                if q == 0:
                    pe.wait_ge(wr_done, 1)
                ps = take(1, logits_read, q + 1)
                for t in range(TPC):
                    o = t * 2 * E
                    tokens = slice((q % CHUNKS * TPC + t) * P, (q % CHUNKS * TPC + t + 1) * P)
                    for j, part in enumerate((xT_hi, xT_lo)):
                        mm = pe.matmul(ps[:, o:o + 2 * E], part[:, tokens],
                                       wr_parts[:, j].rearrange("p k e -> p (k e)"), start=(j == 0), stop=(j == 1))
                mm.then_inc(logits_done, 1)

            def rank(q):
                l, c = q // CHUNKS, q % CHUNKS
                pe.wait_ge(masks_done, q + 1)
                if q == 0:
                    pe.wait_ge(bf_ready, 2)
                ps = take(1, ranks_read, q + 1)
                m = mask[:, l, tiles_of(c), :]
                mm = pe.matmul(ps[:, 0:TPC * E], tri[:], m.rearrange("p t e -> p (t e)"), start=True, stop=True)
                for d in range(1, TPC):
                    mm = pe.matmul(ps[:, d * E:TPC * E], ones[:], m[:, 0:TPC - d, :].rearrange("p t e -> p (t e)"),
                                   start=False, stop=True, skip_group_check=True)
                if c:
                    mm = pe.matmul(ps[:, 0:TPC * E], ones[:], seen[:, q].unsqueeze(1).to_broadcast([P, TPC, E]),
                                   start=False, stop=True, skip_group_check=True)
                mm.then_inc(ranks_done, 1)

            def gathered(le):
                g = gidx(*le)
                ps = take(0, xg_lo_done, g + 1)
                pe.wait_ge(rows_in[g % XG_RING], 32 * (g // XG_RING + 1))
                for j, (r0, n) in enumerate(BLOCKS):
                    mm = pe.transpose(ps[:, r0:r0 + n], xg[0:n, g % XG_RING, j, 0:H], ident[0:n, 0:n])
                mm.then_inc(xg_turned, 1)

            def out_turn(u):
                ps = take(1, out_read, u + 1)
                pe.wait_ge(out_copied, experts_before(u + 1))
                for j, (r0, n) in enumerate(BLOCKS):
                    mm = pe.transpose(ps[0:n, j * P:(j + 1) * P], oT[:, r0:r0 + n], ident)
                mm.then_inc(out_turned, 1)

            def a_turn(c):
                ps = take(0, xaT_done, c + 1)
                pe.wait_ge(xa_done, c + 1)
                for t in range(TPC):
                    mm = pe.transpose(ps[:, t * P:(t + 1) * P], XN[:, c * TPC + t, 0:H], ident)
                mm.then_inc(xa_turned, 1)

            def a_gram(c):
                pe.wait_ge(xa_done, c + 1)
                ps = take(1, gram_sb, c + 1)
                tpb = TPC // BPC
                for b in range(BPC):
                    for t in range(tpb):
                        rows = XN[:, c * TPC + b * tpb + t, 0:H]
                        mm = pe.matmul(ps[:, b * P:(b + 1) * P], rows, rows, start=(t == 0), stop=(t == tpb - 1))
                mm.then_inc(gram_ps, 1)

            def a_gq(c):
                ps = take(0, gq_sb, c + 1)
                pe.wait_ge(gram_sb, c + 1)
                if c == 0:
                    pe.wait_ge(attn_in, 16)
                for b in range(BPC):
                    mm = pe.matmul(ps[:, b * P:(b + 1) * P], gram[:, b, :], wqT, start=True, stop=True)
                mm.then_inc(gq_ps, 1)

            def a_kq(c):
                ps = take(1, kq_read, c + 1)
                pe.wait_ge(gq_sb, c + 1)
                pe.matmul(ps[:, 0:BPC * P], wkT, gq[:].rearrange("p b q -> p (b q)"), start=True, stop=True)\
                    .then_inc(kq_ps, 1)

            def a_pv(c):
                ps = take(0, pv_sb, c + 1)
                pe.wait_ge(zb_done, c + 1)
                for b in range(BPC):
                    mm = pe.matmul(ps[:, b * P:(b + 1) * P], zb[:, b, :], wv, start=True, stop=True)
                mm.then_inc(pv_ps, 1)

            def a_mix(c):
                ps = take(1, mix_sb, c + 1)
                pe.wait_ge(pv_sb, c + 1)
                for b in range(BPC):
                    mm = pe.matmul(ps[:, b * P:(b + 1) * P], pv[:, b, :], woT, start=True, stop=True)
                mm.then_inc(mix_ps, 1)

            def a_out(c):
                ps = take(0, attn_added, c + 1)
                pe.wait_ge(mix_sb, c + 1)
                for t in range(TPC):
                    mm = pe.matmul(ps[:, t * P:(t + 1) * P], xaT[:, c % XA_RING, t * P:(t + 1) * P],
                                   mix[:, t * BPC // TPC, :], start=True, stop=True)
                mm.then_inc(attn_ps, 1)

            do = dict(transpose=transpose, route=route, rank=rank, gathered=gathered, out_turn=out_turn,
                      a_turn=a_turn, a_gram=a_gram, a_gq=a_gq, a_kq=a_kq, a_pv=a_pv, a_mix=a_mix, a_out=a_out)
            pe.wait_ge(const_in, 32)
            for n in range(FIRST, LAST + 1):
                if 0 <= n < NSLOT:
                    gate_up(n)
                for half in range(2):
                    if half == 1 and 2 <= n < NSLOT + 2:
                        down(n - 2)
                    for name, arg in stages[PE].get(2 * n + half, ()):
                        if name in do:
                            do[name](arg)

        @block.scalar
        def _(act):
            act.dma_start(cst[:], consts).then_inc(const_in, 16)
            act.dma_start(wr[:], w_router).then_inc(const_in, 16)
            act.wait_ge(pool_const, 1)
            act.activation(warm[:], mhalf[:], ACT.Silu)

            def normalise(k, c, done):
                for t in range(c * TPC, (c + 1) * TPC):
                    ins = act.activation(XN[:, t, 0:H], X[:, t, :], ACT.Identity,
                                         bias=shift[:, k, t:t + 1], scale=rstd[:, k, t:t + 1])
                ins.then_inc(done, 1)

            def apply(q):
                act.wait_ge(ln_pow, q + 1)
                if q >= CHUNKS:
                    act.wait_ge(gram_ps, q - CHUNKS + 1)
                    act.wait_ge(xa_turned, q - CHUNKS + 1)
                normalise(q // CHUNKS, q % CHUNKS, xn_done)

            def a_apply(c):
                act.wait_ge(an_pow, c + 1)
                if c == 0:
                    act.wait_ge(dispatched[0], 16 * TOP * TILES)
                normalise(LAYERS, c, xa_done)

            def silu(n):
                N = slots[n][4]
                act.wait_ge(gu_done, n + 1)
                if n >= 2:
                    act.wait_ge(hidden_done, n - 1)
                act.activation(S[:, n % 2, 0:N], psG[n % 2][:, 0:N], ACT.Silu).then_inc(silu_done, 1)

            def split(p):
                raw_ready(act, p)
                act.copy(wgu_hi[:, p * PIECE:(p + 1) * PIECE], raw[:, p % RAW_RING, :]).then_inc(hi_split, 1)

            def transpose(q):
                act.wait_ge(xT_turned, q + 1)
                act.copy(xT_hi[:, q % CHUNKS * C:(q % CHUNKS + 1) * C], psM[0][:]).then_inc(xT_hi_done, 1)

            def gate(q):
                act.wait_ge(gap_done, q + 1)
                act.activation(tanh_gap[:, q], gap[:, q], ACT.Tanh).then_inc(tanh_done, 1)
                act.wait_ge(tanh_done, q + 1)
                rows = XN[:, tiles_of(q % CHUNKS), :]
                act.activation(rows[:, :, COL_W1], tanh_gap[:, q], ACT.Identity, bias=quarter[:], scale=-0.25)
                act.activation(rows[:, :, COL_DW], tanh_gap[:, q], ACT.Copy, scale=0.5).then_inc(gates_done, 1)

            def gathered(le):
                g = gidx(*le)
                act.wait_ge(xg_turned, g + 1)
                act.copy(xgT_hi[:, g % 2, :], psM[0][:, 0:CAP]).then_inc(xg_hi_done, 1)

            def out_copy(u):
                N = slots[last_slot[u]][4]
                act.wait_ge(down_done, last_slot[u] + 1)
                if experts_before(u):
                    act.wait_ge(out_turned, experts_before(u))
                act.copy(oT[:], psD[u % 2][:, 0:N]).then_inc(out_copied, 1)

            def a_turn(c):
                act.wait_ge(xa_turned, c + 1)
                if c >= XA_RING:
                    act.wait_ge(attn_ps, c - XA_RING + 1)
                act.copy(xaT[:, c % XA_RING, :], psM[0][:]).then_inc(xaT_done, 1)

            def small(c, ps_done, bank, dst, done, used):
                act.wait_ge(ps_done, c + 1)
                if c:
                    act.wait_ge(used, c)
                act.copy(dst[:].rearrange("p b q -> p (b q)"), psM[bank][:, 0:BPC * P]).then_inc(done, 1)

            def a_gram(c):
                small(c, gram_ps, 1, gram, gram_sb, gq_ps)

            def a_gq(c):
                small(c, gq_ps, 0, gq, gq_sb, kq_ps)

            def a_exp(c):
                act.wait_ge(zs_done, c + 1)
                act.activation(zt[:], zs[:], ACT.Tanh, scale=0.5 * SCALE).then_inc(zt_done, 1)

            def a_pv(c):
                small(c, pv_ps, 0, pv, pv_sb, mix_ps)

            def a_mix(c):
                small(c, mix_ps, 1, mix, mix_sb, attn_ps)

            do = dict(split=split, apply=apply, a_apply=a_apply, transpose=transpose, gate=gate, gathered=gathered, out_copy=out_copy,
                      a_turn=a_turn,
                      a_gram=a_gram, a_gq=a_gq, a_exp=a_exp, a_pv=a_pv, a_mix=a_mix)
            for n in range(FIRST, LAST + 1):
                for half in range(2):
                    if half == 1 and 0 <= n < NSLOT:
                        silu(n)
                    for name, arg in stages[ACTE].get(2 * n + half, ()):
                        if name in do:
                            do[name](arg)

        @block.vector
        def _(dve):
            steps = [0]

            def step(ins):
                steps[0] += 1
                ins.then_inc(dve_step, 1)

            def wait_steps():
                dve.wait_ge(dve_step, steps[0])

            def then(ins):
                step(ins)
                wait_steps()

            def hidden(n):
                N = slots[n][4]
                dve.wait_ge(silu_done, n + 1)
                if n >= H_RING:
                    dve.wait_ge(down_done, n - H_RING + 1)
                dve.tensor_tensor(Hd[:, n % H_RING, 0:N], S[:, n % 2, 0:N], psU[n % 2][:, 0:N], ALU.mult)\
                    .then_inc(hidden_done, 1)

            def split(p):
                dve.wait_ge(hi_split, p + 1)
                cols = slice(p * PIECE, (p + 1) * PIECE)
                dve.tensor_tensor(wgu_lo[:, cols], raw[:, p % RAW_RING, :], wgu_hi[:, cols].bitcast(F32), ALU.subtract)\
                    .then_inc(lo_split, 1)

            def tile_stats(k, c):
                for t in range(c * TPC, (c + 1) * TPC):
                    ins = dve.bn_stats(stat[:, k, t, :], X[:, t, :])
                step(ins)

            def mean_var(k, c, done):
                wait_steps()
                for t in range(c * TPC, (c + 1) * TPC):
                    ins = dve.bn_aggr(mv[:, k, t, :], stat[:, k, t, :])
                then(ins)
                ts = tiles_of(c)
                dve.tensor_scalar(neg_mean[:, k, ts], mv[:, k, ts, 0], -1.0, None, ALU.mult)
                dve.tensor_scalar(var_eps[:, k, ts], mv[:, k, ts, 1], LN_EPS, None, ALU.add).then_inc(done, 1)

            def ln(q):
                if q < CHUNKS:
                    dve.wait_ge(x_in[q], 16)
                tile_stats(q // CHUNKS, q % CHUNKS)

            def ln_var(q):
                mean_var(q // CHUNKS, q % CHUNKS, ln_stats)

            def rms(q):
                l, ts = q // CHUNKS, tiles_of(q % CHUNKS)
                dve.tensor_scalar(msq[:, l, ts], mv[:, l, ts, 1], 4.0 * (1.0 + RMS_EPS), 4.0 * RMS_EPS * LN_EPS, ALU.mult, ALU.add)
                dve.wait_ge(ln_stats, q + 1)
                then(dve.reciprocal(inv_var[:, l, ts], var_eps[:, l, ts]))
                dve.tensor_tensor(msq[:, l, ts], msq[:, l, ts], inv_var[:, l, ts], ALU.mult).then_inc(msq_done, 1)

            def apply(q):
                dve.wait_ge(ln_pow, q + 1)
                dve.wait_ge(pool_const, 3)
                for t in range(TPC):
                    ins = dve.tensor_scalar(XN[:, t, 0:H], X[:, t, :], mv[:, q, t, 0:1], rstd[:, q, t:t + 1],
                                            ALU.subtract, ALU.mult)
                ins.then_inc(xn_done, 1)

            def transpose(q):
                dve.wait_ge(xT_hi_done, q + 1)
                tokens = slice(q % CHUNKS * C, (q % CHUNKS + 1) * C)
                dve.tensor_tensor(xT_lo[:, tokens], psM[0][:], xT_hi[:, tokens].bitcast(F32), ALU.subtract)\
                    .then_inc(xT_lo_done, 1)

            def best(q):
                l, ts = q // CHUNKS, tiles_of(q % CHUNKS)
                dve.wait_ge(logits_done, q + 1)
                dve.tensor_reduce(logit[:], psM[1][:, 0:TPC * 2 * E].rearrange("p (t k e) -> p t e k", k=2, e=E),
                                  AX.X, ALU.add).then_inc(logits_read, 1)
                dve.wait_ge(logits_read, q + 1)
                for t in range(TPC):
                    ins = dve.max(top_v[:, t, :], logit[:, t, :])
                then(ins)
                step(dve.tensor_tensor(gap[:, q], top_v[:, :, 0], top_v[:, :, 1], ALU.subtract))
                for t in range(TPC):
                    ins = dve.max_index(top_i[:, t, :], top_v[:, t, :], logit[:, t, :])
                then(ins)
                step(dve.tensor_tensor(choice[:, q % 2],
                                       iota_e[:].unsqueeze(1).unsqueeze(1).to_broadcast([P, TOP, TPC, E]),
                                       top_i[:, :, 0:TOP].rearrange("p t k -> p k t").unsqueeze(3)
                                       .to_broadcast([P, TOP, TPC, E]), ALU.is_equal))
                step(dve.tensor_copy(XN[:, ts, COL_E0], top_i[:, :, 0]))
                dve.wait_ge(rms_pow, q + 1)
                dve.tensor_tensor(gap[:, q], gap[:, q], half_rrms[:, l, ts], ALU.mult).then_inc(gap_done, 1)

            def choose(q):
                l, ts = q // CHUNKS, tiles_of(q % CHUNKS)
                wait_steps()
                dve.tensor_tensor(mask[:, l, ts], choice[:, q % 2, 0], choice[:, q % 2, 1], ALU.add).then_inc(masks_done, 1)
                if q % CHUNKS < CHUNKS - 1:
                    dve.wait_ge(masks_done, q + 1)
                    with nc.allow_low_precision(reason="counts up to the number of tiles are exact in bfloat16"):
                        step(dve.tensor_reduce(seen[:, q + 1], mask[:, l, 0:ts.stop].rearrange("p t e -> p e t"),
                                               AX.X, ALU.add))

            def rank(q):
                dve.wait_ge(ranks_done, q + 1)
                ps = psM[1][:, 0:TPC * E].rearrange("p (t e) -> p t e", e=E)
                dve.tensor_scalar(late[:], ps, float(CAP), float(FAR), ALU.is_ge, ALU.mult)
                dve.tensor_tensor(place[:], ps, slot_base[:].unsqueeze(1).to_broadcast([P, TPC, E]), ALU.add)\
                    .then_inc(ranks_read, 1)
                dve.wait_ge(ranks_read, q + 1)
                step(dve.tensor_tensor(place[:], place[:], late[:], ALU.add))

            def place_rows(q):
                wait_steps()
                then(dve.tensor_tensor(picked[:], choice[:, q % 2], place[:].unsqueeze(1).to_broadcast([P, TOP, TPC, E]),
                                       ALU.mult))
                then(dve.tensor_reduce(place_f[:], picked[:], AX.X, ALU.add))
                dve.tensor_scalar(place_u[:, q // CHUNKS, :, tiles_of(q % CHUNKS)], place_f[:], float(E * CAP), None, ALU.min)\
                    .then_inc(places_done, 1)

            def gathered(le):
                l, e = le
                g = gidx(l, e)
                r = g % XG_RING
                dve.wait_ge(xg_hi_done, g + 1)
                dve.tensor_tensor(xgT_lo[:, g % 2, :], psM[0][:, 0:CAP], xgT_hi[:, g % 2, :].bitcast(F32), ALU.subtract)\
                    .then_inc(xg_lo_done, 1)
                then(dve.tensor_scalar(wsl[:, r, :], xg[:, r, :, COL_E0], float(e), None, ALU.is_equal))
                then(dve.tensor_tensor(wsl[:, r, :], wsl[:, r, :], xg[:, r, :, COL_DW], ALU.mult))
                then(dve.tensor_tensor(wsl[:, r, :], wsl[:, r, :], xg[:, r, :, COL_W1], ALU.add))

            def out_add(u):
                dve.wait_ge(down_done, last_slot[u] + 1)
                rows = X[:, tiles_of(units[u][2][0]), :].rearrange("p t h -> p (t h)")
                dve.scalar_tensor_tensor(out=rows, in0=psD[u % 2][:], scalar=0.5, in1=rows, op0=ALU.mult, op1=ALU.add)\
                    .then_inc(out_read, 1)
                dve.wait_ge(out_read, u + 1)

            def out_turn(u):
                g = gidx(*units[u][1:])
                dve.wait_ge(out_turned, experts_before(u + 1))
                if g >= 2:
                    dve.wait_ge(added, 16 * NB * (g - 1))
                for j, (r0, n) in enumerate(BLOCKS):
                    ins = dve.tensor_scalar(yw[0:n, g % 2, j, :], psM[1][0:n, j * P:(j + 1) * P],
                                            wsl[0:n, g % XG_RING, j:j + 1], None, ALU.mult)
                ins.then_inc(out_read, 1)

            def add_sums(k, c):
                dve.wait_ge(sums_in[k % 2], 16 * (k // 2 + 1))
                ins = dve.tensor_tensor(X[:, tiles_of(c), :], X[:, tiles_of(c), :], sums[:, k % 2], ALU.add)
                ins.then_inc(combined, 1)
                dve.wait_ge(combined, k + 1)

            def combine(c):
                add_sums(c, c)

            def a_stats(c):
                tile_stats(LAYERS, c)

            def a_var(c):
                mean_var(LAYERS, c, an_stats)

            def finish(c):
                add_sums(CHUNKS + c, c)

            def a_kq(c):
                dve.wait_ge(kq_ps, c + 1)
                dve.tensor_tensor(kq[:], psM[1][:, 0:BPC * P].rearrange("p (b q) -> p b q", b=BPC),
                                  block_mask.unsqueeze(1).to_broadcast([P, BPC, P]), ALU.mult).then_inc(kq_read, 1)
                dve.wait_ge(kq_read, c + 1)
                step(dve.tensor_reduce(zc[:], kq[:].rearrange("p b (g j) -> p b j g", j=HEAD), AX.X, ALU.add))

            def a_own(c):
                wait_steps()
                then(dve.tensor_reduce(zmax[:], zc[:], AX.X, ALU.max))
                dve.tensor_tensor(zs[:], zc[:], zmax[:].unsqueeze(2).to_broadcast([P, BPC, HEAD]), ALU.subtract)\
                    .then_inc(zs_done, 1)

            def a_exp(c):
                dve.wait_ge(zt_done, c + 1)
                then(dve.tensor_scalar(zden[:], zt[:], -1.0, 1.0, ALU.mult, ALU.add))
                then(dve.reciprocal(zden[:], zden[:]))
                step(dve.tensor_scalar(znum[:], zden[:], 2.0, -1.0, ALU.mult, ALU.add))

            def a_norm(c):
                wait_steps()
                then(dve.tensor_reduce(zsum[:], znum[:], AX.X, ALU.add))
                then(dve.reciprocal(zsum[:], zsum[:]))
                if c:
                    dve.wait_ge(pv_ps, c)
                for b in range(BPC):
                    ins = dve.scalar_tensor_tensor(out=zb[:, b, :].rearrange("p (g j) -> p g j", j=HEAD),
                                                   in0=block_mask.rearrange("p (g j) -> p g j", j=HEAD),
                                                   scalar=zsum[:, b:b + 1],
                                                   in1=znum[:, b, :].unsqueeze(1).to_broadcast([P, P // HEAD, HEAD]),
                                                   op0=ALU.mult, op1=ALU.mult)
                ins.then_inc(zb_done, 1)

            def a_out(c):
                dve.wait_ge(attn_ps, c + 1)
                rows = X[:, tiles_of(c), :].rearrange("p t h -> p (t h)")
                ins = dve.tensor_tensor(rows, psM[0][:], rows, ALU.add)
                ins.then_inc(attn_added, 1)
                dve.wait_ge(attn_added, c + 1)

            def start(_):
                dve.wait_ge(const_in, 32)
                dve.tensor_copy(tri[:], cst[:, 2 * P:3 * P]).then_inc(bf_ready, 1)
                dve.memset(ones[:], 1.0).then_inc(bf_ready, 1)
                dve.tensor_copy(wr_parts[:, 0, 0], wr[:]).then_inc(wr_hi_done, 1)
                dve.tensor_copy(wr_parts[:, 1, 0], wr[:])
                dve.memset(zeros[:], 0.0).then_inc(dve_const, 1)
                dve.wait_ge(wr_hi_done, 1)
                dve.wait_ge(dve_const, 1)
                dve.tensor_copy(wr_parts[:, 1, 1], zeros[:, 0:E])
                dve.tensor_tensor(wr_parts[:, 0, 1], wr[:], wr_parts[:, 0, 0].bitcast(F32), ALU.subtract).then_inc(wr_done, 1)

            do = dict(start=start, split=split, ln=ln, ln_var=ln_var, rms=rms, apply=apply, transpose=transpose, best=best, choose=choose,
                      rank=rank, place=place_rows, gathered=gathered, out_add=out_add, out_turn=out_turn, combine=combine, finish=finish,
                      a_stats=a_stats, a_var=a_var, a_kq=a_kq, a_own=a_own, a_exp=a_exp, a_norm=a_norm, a_out=a_out)
            for n in range(FIRST, LAST + 1):
                for half in range(2):
                    if half == 1 and 0 <= n < NSLOT:
                        hidden(n)
                    for name, arg in stages[DVE].get(2 * n + half, ()):
                        if name in do:
                            do[name](arg)

        @block.gpsimd
        def _(pool):
            steps = [0]

            def then(ins):
                steps[0] += 1
                ins.then_inc(pool_step, 1)
                pool.wait_ge(pool_step, steps[0])

            pool.memset(mhalf[:], -0.5).then_inc(pool_const, 1)
            then(pool.memset(init_row[:], 0.0))
            then(pool.memset(quarter[:], 0.25))
            pool.iota(init_row[:, COL_ID:COL_ID + 1].bitcast(U32), pattern=[[0, 1]], base=T, channel_multiplier=1)\
                .then_inc(pool_const, 1)
            then(pool.iota(XN[:, :, COL_ID].bitcast(U32), pattern=[[P, TILES]], base=0, channel_multiplier=1))
            then(pool.iota(iota_e[:], pattern=[[1, E]], base=0, channel_multiplier=0, allow_small_or_imprecise_dtypes=True))
            then(pool.iota(slot_base[:], pattern=[[CAP, E]], base=0, channel_multiplier=0, allow_small_or_imprecise_dtypes=True))
            then(pool.memset(wsl[:], 0.0))
            pool.memset(xg[:], 0.0).then_inc(pool_const, 1)
            pool.wait_ge(pool_const, 3)

            def rsqrt_var(k, c, done):
                ts = tiles_of(c)
                then(pool.tensor_tensor(rstd[:, k, ts], var_eps[:, k, ts], mhalf[:], ALU.pow))
                pool.tensor_tensor(shift[:, k, ts], neg_mean[:, k, ts], rstd[:, k, ts], ALU.mult).then_inc(done, 1)

            def ffn_pow(q):
                pool.wait_ge(ln_stats, q + 1)
                rsqrt_var(q // CHUNKS, q % CHUNKS, ln_pow)

            def ffn_rms(q):
                l, ts = q // CHUNKS, tiles_of(q % CHUNKS)
                pool.wait_ge(msq_done, q + 1)
                pool.tensor_tensor(half_rrms[:, l, ts], msq[:, l, ts], mhalf[:], ALU.pow).then_inc(rms_pow, 1)

            def attn_pow(c):
                pool.wait_ge(an_stats, c + 1)
                rsqrt_var(LAYERS, c, an_pow)

            def dispatch(q, tiles=range(TPC)):
                l, c = q // CHUNKS, q % CHUNKS
                pool.wait_ge(places_done, q + 1)
                pool.wait_ge(gates_done, q + 1)
                if c == 0:
                    pool.wait_ge(rows_init[l], 16)
                for t in tiles:
                    for k in range(TOP):
                        pool.indirect_dma_start(
                            out=rows_dram[l],
                            out_offset=bass.IndirectOffsetOnAxis(ap=place_u[:, l, k, c * TPC + t:c * TPC + t + 1], axis=0),
                            in_=XN[:, c * TPC + t, :], in_offset=None, bounds_check=E * CAP - 1, oob_is_err=False,
                        ).then_inc(dispatched[l], 16)

            def add_outputs(l, e):
                g = gidx(l, e)
                pool.wait_ge(out_read, unit_of[(EXPERT, l, e)] + 1)
                if e == 0:
                    pool.wait_ge(sums_init[l], 16 * (CHUNKS + 1))
                if g:
                    pool.wait_ge(added, 16 * NB * g)
                for j, (r0, n) in enumerate(BLOCKS):
                    pool.indirect_dma_start(
                        out=sums_dram[l],
                        out_offset=bass.IndirectOffsetOnAxis(ap=xg[0:n, g % XG_RING, j, COL_ID:COL_ID + 1].bitcast(U32), axis=0),
                        in_=yw[0:n, g % 2, j, :], in_offset=None, compute_op=ALU.add,
                    ).then_inc(added, 16)

            do = dict(ffn_pow=ffn_pow, ffn_rms=ffn_rms, attn_pow=attn_pow, dispatch=dispatch, add_outputs=add_outputs)
            for name, *args in POOL_STAGES:
                do[name](*args)


def kernel(**inputs):
    import numpy as np
    import concourse.bacc as bacc
    from concourse import mybir as _mybir
    from concourse.bass_utils import run_bass_kernel_spmd

    a = {k: np.asarray(v) for k, v in inputs.items()}
    x = a["L0_attn_x"]
    B, S, H = x.shape
    T = B * S
    E = a["L0_ffn_rg"].shape[0]

    def hidden_last(w):
        w = w.reshape(-1, H, w.shape[-1] // P, P)
        return w.transpose(1, 0, 2, 3).reshape(H, -1, P)

    def hidden_first(w):
        return w.reshape(-1, P, H).transpose(1, 0, 2)

    gate = np.concatenate([hidden_last(a["L0_ffn_sg"]), hidden_last(a["L0_ffn_rg"])], axis=1)
    up = np.concatenate([hidden_last(a["L0_ffn_su"]), hidden_last(a["L0_ffn_ru"])], axis=1)
    down = np.concatenate([hidden_first(a["L0_ffn_sd"]), hidden_first(a["L0_ffn_rd"])], axis=1)
    r = np.arange(P)
    consts = np.concatenate([r[:, None] == r, r[:, None] // 8 == r // 8, r[:, None] < r], axis=1)
    arrays = {
        "x": x.reshape(T, H),
        "w_gate_up": np.stack([gate, up], axis=2).reshape(H, -1),
        "w_down": down.reshape(P, -1),
        "w_attn": np.concatenate([a["L0_attn_Wq"].T, a["L0_attn_Wk"].T, a["L0_attn_Wv"], a["L0_attn_Wo"].T], axis=1),
        "w_router": a["L0_ffn_router_w"].T,
        "consts": consts.astype(np.float32),
    }
    arrays = {k: np.ascontiguousarray(v) for k, v in arrays.items()}
    nc = bacc.Bacc("TRN2", target_bir_lowering=False, num_devices=1)
    args = [nc.dram_tensor(k, v.shape, _mybir.dt.from_np(v.dtype), kind="ExternalInput").ap() for k, v in arrays.items()]
    out = nc.dram_tensor("out", (T, H), _mybir.dt.float32, kind="ExternalOutput").ap()
    macaron_block_kernel(nc, *args, out)
    res = run_bass_kernel_spmd(nc, [arrays], core_ids=[0])
    return res.results[0]["out"].reshape(B, S, H)
```
